# Optimizing a Trainium2 kernel written in Bass

```python
import numpy as np
import jax
import jax.numpy as jnp

def _softmax(x, axis=-1):
    return jax.nn.softmax(x, axis=axis)
def _gelu(x):
    return jax.nn.gelu(x, approximate=True)
def _silu(x):
    return jax.nn.silu(x)
def _sigmoid(x):
    return jax.nn.sigmoid(x)
def _layernorm(x, axis=-1, eps=1e-5):
    m = jnp.mean(x, axis=axis, keepdims=True)
    v = jnp.var(x, axis=axis, keepdims=True)
    return (x - m) / jnp.sqrt(v + eps)
def _scatter_add(tgt, idx, src, axis=0):
    return tgt.at[idx].add(src)
def _segment_sum(src, seg, n):
    return jax.ops.segment_sum(src, seg, n)

kernel_name = 'mk_adj_preln_d2_adj_128_accda6'

def setup_inputs(seed: int = 0):
    np.random.seed(seed)
    _w = jnp.asarray
    def _rec_inputs():
        import jax
        import jax.numpy as jnp
        _gk = jax.random.key(seed)
        x = -0.0005207 + 1.001 * jax.random.normal(jax.random.fold_in(_gk, 1), (3327, 128), jnp.float32)
        _a = jax.random.bernoulli(jax.random.fold_in(_gk, 2), 0.00120228, (3327, 3327))
        _a = jnp.logical_or(_a, jnp.swapaxes(_a, -1, -2))
        _a = jnp.logical_or(_a, jnp.eye(3327, dtype=bool))
        _af = _a.astype(jnp.float32)
        _af = _af * jax.random.uniform(jax.random.fold_in(_gk, 3), (3327, 3327), jnp.float32, 0.05, 1)
        adj = _af
        return x, adj
    x, adj = _rec_inputs()
    def _L0_gnn_setup():
        import jax, jax.numpy as jnp
        import numpy as np
        N = 16384
        IN_DIM = 128
        OUT_DIM = 128

        def _message(X, A, W):
            deg = jnp.sum(A, axis=1, keepdims=True)
            A_norm = A / jnp.where(deg > 0, deg, 1.0)
            return A_norm @ X @ W
        key = jax.random.key(seed)
        k1, k2, k3, k4 = jax.random.split(key, 4)
        X = jax.random.normal(k1, (N, IN_DIM), dtype=jnp.float32)
        A = jax.random.uniform(k2, (N, N), dtype=jnp.float32)
        W_in = jax.random.normal(k3, (IN_DIM, OUT_DIM), dtype=jnp.float32) / np.sqrt(IN_DIM)
        W_out = jax.random.normal(k4, (IN_DIM, OUT_DIM), dtype=jnp.float32) / np.sqrt(IN_DIM)
        return {'X': X, 'A': A, 'W_in': W_in, 'W_out': W_out}
    _L0_gnn_all = _L0_gnn_setup()
    _L0_gnn_in = {k: v for k, v in _L0_gnn_all.items() if k in ('W_in', 'W_out', )}
    del _L0_gnn_all

    def _L1_gnn_setup():
        import jax, jax.numpy as jnp
        import numpy as np
        N = 1024
        D = 128
        H = 8
        key = jax.random.key(seed)
        ks = jax.random.split(key, 7)
        s = (D * H) ** (-0.5)
        return {'x': jax.random.normal(ks[0], (N, D), dtype=jnp.float32), 'spatial_encoding': jax.random.normal(ks[1], (N, N), dtype=jnp.float32), 'edge_encoding': jax.random.normal(ks[2], (N, N), dtype=jnp.float32), 'Wq': jax.random.normal(ks[3], (D * H, D), dtype=jnp.float32) * s, 'Wk': jax.random.normal(ks[4], (D * H, D), dtype=jnp.float32) * s, 'Wv': jax.random.normal(ks[5], (D * H, D), dtype=jnp.float32) * s, 'Wo': jax.random.normal(ks[6], (D, D * H), dtype=jnp.float32) * s}
    _L1_gnn_all = _L1_gnn_setup()
    _L1_gnn_in = {k: v for k, v in _L1_gnn_all.items() if k in ('Wq', 'Wk', 'Wv', 'Wo', )}
    del _L1_gnn_all

    return {
        "x": x,
        "adj": adj,
        "L0_gnn_W_in": _L0_gnn_in["W_in"],
        "L0_gnn_W_out": _L0_gnn_in["W_out"],
        "L1_gnn_Wq": _L1_gnn_in["Wq"],
        "L1_gnn_Wk": _L1_gnn_in["Wk"],
        "L1_gnn_Wv": _L1_gnn_in["Wv"],
        "L1_gnn_Wo": _L1_gnn_in["Wo"],
    }

def reference(x, adj, L0_gnn_W_in, L0_gnn_W_out, L1_gnn_Wq, L1_gnn_Wk, L1_gnn_Wv, L1_gnn_Wo):
    import jax
    import jax.numpy as jnp
    def _L0_gnn_ref(X, A, W_in, W_out):
        import jax, jax.numpy as jnp
        import numpy as np
        N = 16384
        IN_DIM = 128
        OUT_DIM = 128

        def _message(X, A, W):
            deg = jnp.sum(A, axis=1, keepdims=True)
            A_norm = A / jnp.where(deg > 0, deg, 1.0)
            return A_norm @ X @ W
        X_in = _message(X, A, W_in)
        X_out = _message(X, A.T, W_out)
        return X_in + X_out

    def _L1_gnn_ref(x, spatial_encoding, edge_encoding, Wq, Wk, Wv, Wo):
        import jax, jax.numpy as jnp
        import numpy as np
        N = 1024
        D = 128
        H = 8
        n, d = x.shape
        h = Wq.shape[0] // d
        scale = d ** (-0.5)
        q = (x @ Wq.T).reshape(d, n, h)
        k = (x @ Wk.T).reshape(d, n, h)
        v = (x @ Wv.T).reshape(d, n, h)
        a = jnp.einsum('dnh,dmh->dnm', q, k) * scale
        a = a + spatial_encoding + edge_encoding
        a = jax.nn.softmax(a, axis=2)
        out = jnp.einsum('dnm,dmh->dnh', a, v)
        out = out.reshape(n, h * d)
        return out @ Wo.T

    h = jnp.maximum(_layernorm(x, axis=-1), 0.0)
    x = x + _L0_gnn_ref(h, adj, L0_gnn_W_in, L0_gnn_W_out)
    h = jnp.maximum(_layernorm(x, axis=-1), 0.0)
    x = x + _L1_gnn_ref(h, adj, adj, L1_gnn_Wq, L1_gnn_Wk, L1_gnn_Wv, L1_gnn_Wo)
    return x


_drawn_inputs = setup_inputs


def setup_inputs(seed=0):
    import zlib

    import numpy as np

    out = dict(_drawn_inputs(seed))
    spreads = {}
    factors = {'L1_gnn_Wq': 8.0, 'L1_gnn_Wk': 8.0, 'L1_gnn_Wv': 4.553, 'L1_gnn_Wo': 5.71}
    for name, (base, spread) in spreads.items():
        noise = np.random.default_rng([zlib.crc32(name.encode()), seed]).standard_normal(out[name].shape)
        drawn = base * np.exp(spread * noise) if base else spread * noise
        out[name] = jnp.asarray(drawn.astype(out[name].dtype))
    for name, factor in factors.items():
        out[name] = (out[name] * factor).astype(out[name].dtype)
    return out
```

```python
from contextlib import ExitStack

import concourse.bass as bass
from concourse import mybir

ALU = mybir.AluOpType
ACT = mybir.ActivationFunctionType
F32 = mybir.dt.float32
BF16 = mybir.dt.bfloat16
I32 = mybir.dt.int32
AX_X = mybir.AxisListType.X

P = 128
N = 3327
F = 128
H = 8
HEADS = 128
C = -(-N // P)
NP = C * P
LAST = N - (C - 1) * P
TOK = NP * P
BANK = 512
EPS = 1e-5
SCALE = float(F) ** -0.5

BLOCKS = 3
NB = N // BLOCKS
assert NB * BLOCKS == N
PARTS = 3
PROD = PARTS * PARTS * H
SHIFT_ROW = 96
VW = H + 1
COLT = 4
QW = -(-NB // COLT)
QS = NB // COLT
RING = 4
PAIR = 2
LIMIT = 30.0


def row_pieces(total):
    whole = total // 16 * 16
    return [(0, whole)] + ([(whole, total)] if total > whole else [])


def col_pieces(width):
    return [(a, min(a + BANK, width)) for a in range(0, width, BANK)]


def normalise(dve, x, h, centred, stats, chain, rooted, variance_ready, root_count):
    step = chain
    dve.tensor_reduce(stats[:, 0, :], x, AX_X, ALU.add).then_inc(step.sem, 1)
    step.done()
    dve.tensor_scalar(stats[:, 0, :], stats[:, 0, :], 1.0 / F, None, ALU.mult).then_inc(step.sem, 1)
    step.done()
    for c in range(C):
        last = dve.tensor_scalar(centred[:, c, :], x[:, c, :], stats[:, 0, c:c + 1], None, ALU.subtract)
    last.then_inc(step.sem, 1)
    step.done()
    dve.tensor_tensor(h, centred[:], centred[:], ALU.mult).then_inc(step.sem, 1)
    step.done()
    dve.tensor_reduce(stats[:, 1, :], h, AX_X, ALU.add).then_inc(step.sem, 1)
    step.done()
    dve.tensor_scalar(stats[:, 1, :], stats[:, 1, :], 1.0 / F, EPS, ALU.mult, ALU.add).then_inc(variance_ready, 1)
    dve.wait_ge(rooted, root_count)
    dve.reciprocal(stats[:, 3, :], stats[:, 2, :]).then_inc(step.sem, 1)
    step.done()
    for c in range(C):
        last = dve.tensor_scalar(h[:, c, :], centred[:, c, :], stats[:, 3, c:c + 1], 0.0, ALU.mult, ALU.max)
    last.then_inc(step.sem, 1)
    step.done()


class Chain:

    def __init__(self, engine, sem):
        self.engine, self.sem, self.count = engine, sem, 0

    def done(self):
        self.count += 1
        self.engine.wait_ge(self.sem, self.count)


class Scope:

    def __init__(self, nc, ctx, tag):
        self.nc, self.ctx, self.tag = nc, ctx, tag

    def sb(self, name, shape, dt=F32):
        return self.ctx.enter_context(self.nc.sbuf_tensor(f"{self.tag}_{name}", shape, dt))

    def ps(self, name, shape, dt=F32):
        return self.ctx.enter_context(self.nc.psum_tensor(f"{self.tag}_{name}", shape, dt))

    def sem(self, name):
        return self.ctx.enter_context(self.nc.semaphore(f"{self.tag}_{name}"))


def load_and_norm_first(nc, x, keep):
    with ExitStack() as ctx:
        s = Scope(nc, ctx, "n1")
        x_int = s.sb("x_int", [P, C, F])
        centred = s.sb("centred", [P, C, F])
        stats = s.sb("stats", [P, 4, C])
        cleared, x_loaded = s.sem("cleared"), s.sem("x_loaded")
        variance_ready, rooted, steps = s.sem("variance_ready"), s.sem("rooted"), s.sem("steps")
        ident_zero, ident_done = s.sem("ident_zero"), s.sem("ident_done")
        x_nat = keep["x"]
        block = ctx.enter_context(nc.Block())
        loads = 1 + 2 * len(row_pieces(LAST)) + 1

        @block.sync
        def _(sp):
            sp.wait_ge(cleared, 2)
            sp.dma_start(x_nat[:, 0:C - 1, :], x[0:(C - 1) * P, :].rearrange("(c p) f -> p c f", p=P)).then_inc(x_loaded, 16)
            for a, b in row_pieces(LAST):
                sp.dma_start(x_nat[a:b, C - 1, :], x[(C - 1) * P + a:(C - 1) * P + b, :]).then_inc(x_loaded, 16)
                sp.dma_start(x_int[a:b, :, :], x[C * a:C * b, :].rearrange("(p j) f -> p j f", j=C)).then_inc(x_loaded, 16)
            sp.dma_start(x_int[P - 1:P, 0:C - 1, :],
                         x[C * (P - 1):N, :].rearrange("(p j) f -> p j f", p=1)).then_inc(x_loaded, 16)

        @block.gpsimd
        def _(pool):
            pool.memset(keep["ident"][:], 0.0).then_inc(ident_zero, 1)
            pool.wait_ge(ident_zero, 1)
            pool.affine_select(out=keep["ident"][:], in_=keep["ident"][:], compare_op=ALU.not_equal, fill=1.0,
                               base=0, pattern=[[-1, P]], channel_multiplier=1).then_inc(ident_done, 1)

        @block.scalar
        def _(act):
            for k in range(2):
                act.wait_ge(variance_ready, k + 1)
                act.activation(stats[:, 2, :], stats[:, 1, :], ACT.Sqrt).then_inc(rooted, 1)

        @block.vector
        def _(dve):
            dve.memset(keep["ones"][:], 1.0)
            dve.memset(x_nat[:, C - 1, :], 0.0).then_inc(cleared, 1)
            dve.memset(x_int[:, C - 1, :], 0.0).then_inc(cleared, 1)
            dve.wait_ge(x_loaded, 16 * loads)
            chain = Chain(dve, steps)
            normalise(dve, x_nat[:], keep["h_nat"][:], centred, stats, chain, rooted, variance_ready, 1)
            normalise(dve, x_int[:], keep["h_int"][:], centred, stats, chain, rooted, variance_ready, 2)


def stream_adjacency(nc, adj, at_d, amax_d, keep):
    with ExitStack() as ctx:
        s = Scope(nc, ctx, "st")
        a_rows = [s.sb(f"a_rows{k}", [P, NP]) for k in range(2)]
        a_t = [s.sb(f"a_t{k}", [P, C, P]) for k in range(2)]
        h_now = [s.sb(f"h_now{k}", [P, F]) for k in range(2)]
        zero_row = s.sb("zero_row", [1, NP])
        row_max = s.sb("row_max", [P, C])
        tp = [s.ps(f"tp{k}", [P, BANK]) for k in range(2)]
        out_sum = [s.ps(f"out_sum{k}", [P, BANK]) for k in range(2)]
        in_sum = [s.ps(f"in_sum{k}", [P, BANK]) for k in range(2)]
        cleared = s.sem("cleared")
        a_loaded = [s.sem(f"a_loaded{k}") for k in range(2)]
        last_loaded, max_stored = s.sem("last_loaded"), s.sem("max_stored")
        h_copied, at_copied = s.sem("h_copied"), s.sem("at_copied")
        at_stored = [s.sem(f"at_stored{k}") for k in range(2)]
        transposed, out_ready, out_added = s.sem("transposed"), s.sem("out_ready"), s.sem("out_added")
        in_ready, in_copied = s.sem("in_ready"), s.sem("in_copied")
        dve_read, pool_added, out_zero = s.sem("dve_read"), s.sem("pool_added"), s.sem("out_zero")
        block = ctx.enter_context(nc.Block())
        groups = [range(g, min(g + 4, C)) for g in range(0, C, 4)]
        G = len(groups)
        pieces = col_pieces(NP)
        assert len(pieces) == G
        FREE = 2

        @block.sync
        def _(sp):
            def load(c, k):
                sp.dma_start(a_rows[k][:, 0:N], bass.AP(adj.tensor, c * (P * N), [[N, P], [1, N]])).then_inc(a_loaded[k], 16)

            def store(c, k):
                sp.wait_ge(at_copied, G * c + G + FREE)
                sp.dma_start(bass.AP(at_d, c * P, [[C * NP, P], [NP, C], [1, P]]), a_t[k][:]).then_inc(at_stored[k], 16)

            def all_read(c):
                sp.wait_ge(in_ready, c + 1 + FREE)
                sp.wait_ge(dve_read, c + 1 + FREE)
                sp.wait_ge(pool_added, c + 1 + FREE)

            for k in range(2):
                sp.sem_inc(at_stored[k], 16)
            sp.wait_ge(cleared, 3)
            load(0, 0)
            load(1, 1)
            with sp.Fori(0, C // 2 - 2) as i:
                for k in range(2):
                    store(2 * i + k, k)
                    all_read(2 * i + k)
                    load(2 * i + k + 2, k)
            store(C - 4, 0)
            all_read(C - 4)
            load(C - 2, 0)
            store(C - 3, 1)
            all_read(C - 3)
            (_, whole), (_, rest) = row_pieces(LAST)
            sp.dma_start(a_rows[1][LAST:P, :], zero_row[:]).then_inc(last_loaded, 16)
            sp.dma_start(a_rows[1][whole:rest, 0:N], adj[(C - 1) * P + whole:N, :]).then_inc(last_loaded, 16)
            sp.wait_ge(last_loaded, 32)
            sp.dma_start(a_rows[1][0:whole, 0:N], adj[(C - 1) * P:(C - 1) * P + whole, :]).then_inc(a_loaded[1], 16)
            store(C - 2, 0)
            store(C - 1, 1)
            sp.wait_ge(dve_read, C + FREE)
            sp.dma_start(bass.AP(amax_d, 0, [[1, P], [P, C], [1, 1]]), row_max[:].rearrange("p (c o) -> p c o", o=1),
                         allow_slow_non_contiguous=True).then_inc(max_stored, 16)
            sp.wait_ge(max_stored, 16)
            for k in range(2):
                sp.wait_ge(at_stored[k], 16 * (C // 2) + 16)

        @block.gpsimd
        def _(pool):
            pool.memset(zero_row[:], 0.0).then_inc(cleared, 1)
            pool.memset(keep["col_acc"][:], 0.0).then_inc(pool_added, FREE)
            with pool.Fori(0, C // 2) as i:
                for k in range(2):
                    c = 2 * i + k
                    pool.wait_ge(in_ready, c + 1)
                    pool.tensor_copy(h_now[k][:], keep["h_nat"][:, c, :]).then_inc(h_copied, 1)
                    pool.wait_ge(a_loaded[k], 16 * i + 16)
                    pool.wait_ge(pool_added, c + FREE)
                    pool.tensor_tensor(keep["col_acc"][:], keep["col_acc"][:], a_rows[k][:], ALU.add).then_inc(pool_added, 1)

        @block.tensor
        def _(pe):
            pe.sem_inc(in_ready, FREE)
            with pe.Fori(0, C // 2) as i:
                for k in range(2):
                    c = 2 * i + k
                    a_cols = a_rows[k][:].rearrange("p (q j) -> p j q", j=C)
                    pe.wait_ge(a_loaded[k], 16 * i + 16)
                    pe.wait_ge(h_copied, c + 1)
                    for g in range(G + 1):
                        if g < G:
                            pe.wait_ge(at_copied, G * c + g + 1)
                            for m, j in enumerate(groups[g]):
                                last = pe.transpose(tp[(G * k + g) % 2][:, m * P:(m + 1) * P], a_cols[:, j, :], keep["ident"][:])
                            last.then_inc(transposed, 1)
                            a, b = pieces[g]
                            pe.wait_ge(out_added, G * c + g + 1)
                            pe.matmul(out_sum[(G * k + g) % 2][:, 0:b - a], h_now[k][:], a_rows[k][:, a:b],
                                      start=True, stop=True).then_inc(out_ready, 1)
                        if g == 0:
                            continue
                        if g == 1:
                            pe.wait_ge(in_copied, c + 1)
                        pe.wait_ge(at_copied, G * c + g + FREE)
                        for j in groups[g - 1]:
                            last = pe.matmul(in_sum[k][:, 0:P], keep["h_int"][:, j, :], a_t[k][:, j, :],
                                             start=(j == 0), stop=(j == C - 1))
                    last.then_inc(in_ready, 1)

        @block.scalar
        def _(act):
            act.sem_inc(at_copied, FREE)
            act.sem_inc(in_copied, FREE)
            with act.Fori(0, C // 2) as i:
                for k in range(2):
                    c = 2 * i + k
                    act.wait_ge(in_ready, c + 1)
                    act.wait_ge(at_stored[k], 16 * i + 16)
                    for g in range(G):
                        j0, n = groups[g][0], len(groups[g])
                        act.wait_ge(transposed, G * c + g + 1)
                        act.activation(a_t[k][:, j0:j0 + n, :].rearrange("p j n -> p (j n)"), tp[(G * k + g) % 2][:, 0:n * P],
                                       ACT.Copy).then_inc(at_copied, 1)
                    act.wait_ge(in_ready, c + 1 + FREE)
                    act.activation(keep["in_acc"][:, bass.ds(c * P, P)], in_sum[k][:, 0:P], ACT.Copy).then_inc(in_copied, 1)

        @block.vector
        def _(dve):
            dve.sem_inc(out_added, FREE)
            dve.sem_inc(dve_read, FREE)
            for k in range(2):
                dve.memset(a_rows[k][:, N:NP], 0.0).then_inc(cleared, 1)
            dve.memset(keep["out_acc"][:], 0.0).then_inc(out_zero, 1)
            dve.wait_ge(out_zero, 1)
            with dve.Fori(0, C // 2) as i:
                for k in range(2):
                    c = 2 * i + k
                    dve.wait_ge(a_loaded[k], 16 * i + 16)
                    dve.tensor_reduce(keep["row_sum"][:, bass.ds(c, 1)], a_rows[k][:], AX_X, ALU.add)
                    dve.tensor_reduce(row_max[:, bass.ds(c, 1)], a_rows[k][:], AX_X, ALU.max,
                                      apply_absolute_value=True).then_inc(dve_read, 1)
                    for g in range(G):
                        a, b = pieces[g]
                        dve.wait_ge(out_ready, G * c + g + 1)
                        dve.wait_ge(out_added, G * c + g + 1)
                        dve.tensor_tensor(keep["out_acc"][:, a:b], keep["out_acc"][:, a:b],
                                          out_sum[(G * k + g) % 2][:, 0:b - a], ALU.add).then_inc(out_added, 1)


def finish_first_layer(nc, w_in, w_out, wq, wk, wv, wo, keep):
    with ExitStack() as ctx:
        s = Scope(nc, ctx, "fl")
        mix = s.sb("mix", [P, 2, F])
        w_nat = s.sb("w_nat", [P, 3, H, F])
        wo_nat = s.sb("wo_nat", [P, H * P])
        centred = s.sb("centred", [P, C, F])
        stats = s.sb("stats", [P, 4, C])
        degree = s.sb("degree", [P, 4, 2, C])
        y = s.ps("y", [P, 8 * BANK])
        deg = y[:, 7 * BANK:7 * BANK + C]
        loaded, deg_ready, rdeg_ready = s.sem("loaded"), s.sem("deg_ready"), s.sem("rdeg_ready")
        mixed, x_ready, steps = s.sem("mixed"), s.sem("x_ready"), s.sem("steps")
        variance_ready, rooted = s.sem("variance_ready"), s.sem("rooted")
        h_ready, h_turned, h_kept, w_turned = s.sem("h_ready"), s.sem("h_turned"), s.sem("h_kept"), s.sem("w_turned")
        block = ctx.enter_context(nc.Block())
        x1, ident = keep["x"], keep["ident"]

        @block.sync
        def _(sp):
            sp.dma_start(mix[:, 0, :], w_in).then_inc(loaded, 16)
            sp.dma_start(mix[:, 1, :], w_out).then_inc(loaded, 16)
            for k, w in enumerate((wq, wk, wv)):
                sp.dma_start(w_nat[:, k, :, :], w.rearrange("(t h) f -> t h f", h=H)).then_inc(loaded, 16)
            sp.dma_start(wo_nat[:], wo).then_inc(loaded, 16)

        @block.tensor
        def _(pe):
            for c in range(C):
                last = pe.matmul(deg[:, c:c + 1], keep["col_acc"][:, c * P:(c + 1) * P], keep["ones"][:, 0:1],
                                 start=True, stop=True)
            last.then_inc(deg_ready, 1)
            pe.wait_ge(loaded, 16 * 6)
            for k, acc in enumerate((keep["in_acc"], keep["out_acc"])):
                if k:
                    pe.wait_ge(x_ready, 1)
                for c in range(C):
                    last = pe.matmul(y[:, c * P:(c + 1) * P], acc[:, c * P:(c + 1) * P], mix[:, k, :], start=True, stop=True)
                last.then_inc(mixed, 1)
            pe.wait_ge(h_ready, 1)
            for c in range(C):
                last = pe.transpose(y[:, c * P:(c + 1) * P], keep["h_nat"][:, c, :], ident[:])
            last.then_inc(h_turned, 1)
            pe.wait_ge(h_kept, 2)
            for k in range(3):
                for h in range(H):
                    at = (k * H + h) * P
                    last = pe.transpose(y[:, at:at + P], w_nat[:, k, h, :], ident[:])
            wo_cols = wo_nat[:].rearrange("o (t h) -> o h t", h=H)
            for h in range(H):
                at = (3 * H + h) * P
                last = pe.transpose(y[:, at:at + P], wo_cols[:, h, :], ident[:])
            last.then_inc(w_turned, 1)

        @block.scalar
        def _(act):
            act.wait_ge(variance_ready, 1)
            act.activation(stats[:, 2, :], stats[:, 1, :], ACT.Sqrt).then_inc(rooted, 1)
            act.wait_ge(h_turned, 1)
            act.activation(keep["h_t"][:, 4 * BANK:NP], y[:, 4 * BANK:NP], ACT.Copy).then_inc(h_kept, 1)
            act.wait_ge(w_turned, 1)
            act.activation(keep["w_t"][:, 4 * BANK:], y[:, 4 * BANK:6 * BANK], ACT.Copy)
            act.activation(keep["wo_t"][:].rearrange("p h o -> p (h o)"), y[:, 6 * BANK:8 * BANK], ACT.Copy)

        @block.vector
        def _(dve):
            chain = Chain(dve, steps)
            dve.tensor_copy(degree[:, 0, 0, :], keep["row_sum"][:])
            dve.wait_ge(deg_ready, 1)
            dve.tensor_copy(degree[:, 0, 1, :], deg).then_inc(steps, 1)
            chain.done()
            dve.tensor_scalar(degree[:, 1, :, :], degree[:, 0, :, :], 0.0, None, ALU.is_gt).then_inc(steps, 1)
            chain.done()
            dve.tensor_tensor(degree[:, 2, :, :], degree[:, 0, :, :], degree[:, 1, :, :], ALU.mult)
            dve.tensor_scalar(degree[:, 3, :, :], degree[:, 1, :, :], -1.0, 1.0, ALU.mult, ALU.add).then_inc(steps, 1)
            chain.done()
            dve.tensor_tensor(degree[:, 0, :, :], degree[:, 2, :, :], degree[:, 3, :, :], ALU.add).then_inc(steps, 1)
            chain.done()
            dve.reciprocal(degree[:, 1, :, :], degree[:, 0, :, :]).then_inc(steps, 1)
            chain.done()
            for k in range(2):
                dve.wait_ge(mixed, k + 1)
                for c in range(C):
                    last = dve.scalar_tensor_tensor(out=x1[:, c, :], in0=y[:, c * P:(c + 1) * P], scalar=degree[:, 1, k, c:c + 1],
                                                    in1=x1[:, c, :], op0=ALU.mult, op1=ALU.add)
                last.then_inc(x_ready, 1)
                dve.wait_ge(x_ready, k + 1)
            normalise(dve, x1[:], keep["h_nat"][:], centred, stats, chain, rooted, variance_ready, 1)
            dve.sem_inc(h_ready, 1)
            dve.wait_ge(h_turned, 1)
            dve.tensor_copy(keep["h_t"][:, 0:4 * BANK], y[:, 0:4 * BANK]).then_inc(h_kept, 1)
            dve.wait_ge(w_turned, 1)
            dve.tensor_copy(keep["w_t"][:, 0:4 * BANK], y[:, 0:4 * BANK])


def project(nc, qp_d, kp_d, v_d, nq_d, nk_d, keep):
    with ExitStack() as ctx:
        s = Scope(nc, ctx, "pr")
        W = H * P
        parts = [[s.sb(f"parts{kind}{k}", [P, PARTS, W], BF16) for kind in "qk"] for k in range(2)]
        rest = [s.sb(f"rest{kind}", [P, W]) for kind in "qk"]
        squares = [s.sb(f"squares{kind}", [P, W]) for kind in "qk"]
        value = [s.sb(f"value{k}", [P, P, VW]) for k in range(2)]
        norm2 = [s.sb(f"norm2{kind}", [P, C, P]) for kind in "qk"]
        h_now = [s.sb(f"h_now{k}", [P, P]) for k in range(2)]
        zeros, zeros_set = s.sb("zeros", [P, W]), s.sem("zeros_set")
        py = [s.ps(f"py{kind}", [P, W]) for kind in "qkv"]
        h_copied, product = s.sem("h_copied"), [s.sem(f"product_{kind}") for kind in "qkv"]
        rest_left, part2, part3 = [[s.sem(f"{n}_{kind}") for kind in "qk"] for n in ("rest_left", "part2", "part3")]
        squared, summed = [[s.sem(f"{n}_{kind}") for kind in "qk"] for n in ("squared", "summed")]
        value_kept, ones_set, rooted, norm_stored = s.sem("value_kept"), s.sem("ones_set"), s.sem("rooted"), s.sem("norm_stored")
        parts_stored = [s.sem(f"parts_stored{k}") for k in range(2)]
        value_stored = [s.sem(f"value_stored{k}") for k in range(2)]
        block = ctx.enter_context(nc.Block())
        PS = 16 * 2 * PARTS

        @block.sync
        def _(sp):
            for k in range(2):
                sp.sem_inc(parts_stored[k], PS)
                sp.sem_inc(value_stored[k], 16)
            with sp.Fori(0, C // 2) as i:
                for k in range(2):
                    c = 2 * i + k
                    for kind, dst in enumerate((qp_d, kp_d)):
                        sp.wait_ge(part3[kind], c + 2)
                        for part in range(PARTS):
                            sp.dma_start(bass.AP(dst, part * H * TOK + c * (P * P), [[P, P], [TOK, H], [1, P]]),
                                         parts[k][kind][:, part, :].rearrange("p (h t) -> p h t", h=H)).then_inc(parts_stored[k], 16)
                    sp.wait_ge(value_kept, c + 2)
                    sp.dma_start(bass.AP(v_d, c * (P * P * VW), [[P * VW, P], [1, P * VW]]),
                                 value[k][:].rearrange("p t v -> p (t v)")).then_inc(value_stored[k], 16)
            sp.wait_ge(rooted, 2)
            for kind, dst in enumerate((nq_d, nk_d)):
                sp.dma_start(bass.AP(dst, 0, [[P, P], [P * P, C], [1, P]]), norm2[kind][:]).then_inc(norm_stored, 16)
            sp.wait_ge(norm_stored, 32)
            for k in range(2):
                sp.wait_ge(parts_stored[k], PS * (C // 2) + PS)
                sp.wait_ge(value_stored[k], 16 * (C // 2) + 16)

        @block.gpsimd
        def _(pool):
            pool.memset(zeros[:], 0.0).then_inc(zeros_set, 1)
            pool.wait_ge(zeros_set, 1)
            for kind in range(2):
                pool.sem_inc(part3[kind], 1)
            with pool.Fori(0, C // 2) as i:
                for k in range(2):
                    c = 2 * i + k
                    pool.wait_ge(product[2], c + 1)
                    pool.tensor_copy(h_now[k][:], keep["h_t"][:, bass.ds(c * P, P)]).then_inc(h_copied, 1)
                    for kind in range(2):
                        pool.wait_ge(rest_left[kind], c + 2)
                        pool.tensor_tensor(parts[k][kind][:, 1, :], rest[kind][:], zeros[:], ALU.add).then_inc(part2[kind], 1)
                        pool.wait_ge(part2[kind], c + 1)
                        pool.tensor_tensor(parts[k][kind][:, 2, :], rest[kind][:], parts[k][kind][:, 1, :],
                                           ALU.subtract).then_inc(part3[kind], 1)

        @block.tensor
        def _(pe):
            pe.sem_inc(product[2], 2)
            with pe.Fori(0, C // 2) as i:
                for k in range(2):
                    c = 2 * i + k
                    pe.wait_ge(h_copied, c + 1)
                    for kind in range(3):
                        if kind < 2:
                            pe.wait_ge(rest_left[kind], c + 1)
                            pe.wait_ge(squared[kind], c + 1)
                        else:
                            pe.wait_ge(value_kept, c + 1)
                        for b in range(0, W, BANK):
                            last = pe.matmul(py[kind][:, b:b + BANK], h_now[k][:], keep["w_t"][:, kind * W + b:kind * W + b + BANK],
                                             start=True, stop=True)
                        last.then_inc(product[kind], 1)

        @block.scalar
        def _(act):
            for kind in range(2):
                act.sem_inc(squared[kind], 1)
            act.sem_inc(value_kept, 1)
            act.wait_ge(ones_set, 2)
            with act.Fori(0, C // 2) as i:
                for k in range(2):
                    c = 2 * i + k
                    act.wait_ge(parts_stored[k], PS * i + PS)
                    for kind in range(2):
                        act.wait_ge(product[kind], c + 1)
                        act.activation(parts[k][kind][:, 0, :], py[kind][:], ACT.Copy, scale=(SCALE, 1.0)[kind])
                        act.wait_ge(summed[kind], c + 1)
                        act.activation(squares[kind][:], py[kind][:], ACT.Square).then_inc(squared[kind], 1)
                    act.wait_ge(product[2], c + 3)
                    act.wait_ge(value_stored[k], 16 * i + 16)
                    act.activation(value[k][:, :, 0:H].rearrange("p t h -> p h t"),
                                   py[2][:].rearrange("p (h t) -> p h t", h=H), ACT.Copy).then_inc(value_kept, 1)
            for kind in range(2):
                act.wait_ge(summed[kind], C + 1)
                act.activation(norm2[kind][:], norm2[kind][:], ACT.Sqrt, scale=(SCALE * SCALE, 1.0)[kind]).then_inc(rooted, 1)

        @block.vector
        def _(dve):
            for k in range(2):
                dve.memset(value[k][:], 1.0).then_inc(ones_set, 1)
            for kind in range(2):
                dve.sem_inc(rest_left[kind], 1)
                dve.sem_inc(summed[kind], 1)
            with dve.Fori(0, C // 2) as i:
                for k in range(2):
                    c = 2 * i + k
                    for kind in range(2):
                        dve.wait_ge(squared[kind], c + 2)
                        dve.wait_ge(part3[kind], c + 1)
                        dve.scalar_tensor_tensor(out=rest[kind][:], in0=py[kind][:], scalar=(SCALE, 1.0)[kind],
                                                 in1=parts[k][kind][:, 0, :], op0=ALU.mult,
                                                 op1=ALU.subtract).then_inc(rest_left[kind], 1)
                        dve.tensor_reduce(norm2[kind][:, c, :], squares[kind][:].rearrange("p (h t) -> p t h", h=H),
                                          AX_X, ALU.add).then_inc(summed[kind], 1)


def bound_scores(nc, nq_d, nk_d, amax_d, shift, over):
    with ExitStack() as ctx:
        s = Scope(nc, ctx, "bo")
        nq, nk, amax = s.sb("nq", [P, N]), s.sb("nk", [P, N]), s.sb("amax", [P, N])
        small, turned = s.sb("small", [P, 2]), s.sb("turned", [1, P + 2])
        loaded, steps, top_ready, top_turned, top_stored = [s.sem(n) for n in ("loaded", "steps", "top_ready", "top_turned", "top_stored")]
        top_d = nc.dram_tensor("top_scratch", (P,), F32)
        block = ctx.enter_context(nc.Block())

        @block.sync
        def _(sp):
            for dst, src, step in ((nq, nq_d, N), (nk, nk_d, N), (amax, amax_d, 0)):
                sp.dma_start(dst[:], bass.AP(src, 0, [[step, HEADS], [1, N]])).then_inc(loaded, 16)
            sp.wait_ge(top_ready, 1)
            sp.dma_start(bass.AP(top_d, 0, [[1, P], [1, 1]]), small[:, 1:2]).then_inc(top_stored, 16)
            sp.wait_ge(top_stored, 16)
            sp.dma_start(turned[:, 0:P], bass.AP(top_d, 0, [[P, 1], [1, P]])).then_inc(top_turned, 16)

        @block.vector
        def _(dve):
            chain = Chain(dve, steps)
            dve.wait_ge(loaded, 48)
            dve.memset(shift[:, N:NP], 0.0)
            dve.tensor_reduce(small[:, 0:1], nk[:], AX_X, ALU.max)
            dve.tensor_scalar(amax[:], amax[:], 2.0, None, ALU.mult).then_inc(steps, 1)
            chain.done()
            dve.scalar_tensor_tensor(out=shift[:, 0:N], in0=nq[:], scalar=small[:, 0:1], in1=amax[:], op0=ALU.mult,
                                     op1=ALU.add).then_inc(steps, 1)
            chain.done()
            dve.tensor_reduce(small[:, 1:2], shift[:, 0:N], AX_X, ALU.max).then_inc(top_ready, 1)
            dve.wait_ge(top_turned, 16)
            dve.tensor_reduce(turned[:, P:P + 1], turned[:, 0:P], AX_X, ALU.max).then_inc(steps, 1)
            chain.done()
            dve.tensor_scalar(turned[:, P + 1:P + 2], turned[:, P:P + 1], LIMIT, None, ALU.is_gt).then_inc(steps, 1)
            chain.done()
            dve.tensor_copy(over[:], turned[:, P + 1:P + 2])


def take_true_maxima(nc, adj, qp_d, kp_d, shift, over, ident):
    with ExitStack() as ctx:
        s = Scope(nc, ctx, "mx")
        a_rows = s.sb("a_rows", [P, N])
        q = s.sb("q", [P, P], BF16)
        k_all = s.sb("k_all", [P, N], BF16)
        scores = s.sb("scores", [P, N])
        tops = s.sb("tops", [P, HEADS])
        py = s.ps("py", [P, 7 * BANK])
        turn = s.ps("turn", [P, P])
        q_now = s.sb("q_now", [P, P], BF16)
        a_loaded, qk_loaded, product, added, top = [s.sem(n) for n in ("a_loaded", "qk_loaded", "product", "added", "top")]
        turned, kept, zeroed, q_zero = s.sem("turned"), s.sem("kept"), s.sem("zeroed"), s.sem("q_zero")
        block = ctx.enter_context(nc.Block())
        LOADS = 16 * (3 + 9)

        def rows_of(c):
            return P if c < C - 1 else LAST

        @block.sync
        def _(sp):
            flag = sp.value_load(over[0:1, 0:1], min_val=0, max_val=1)
            with sp.If(flag != 0):
                sp.wait_ge(zeroed, 2)
                for c in range(C):
                    if c:
                        sp.wait_ge(kept, c)
                    for a, b in row_pieces(rows_of(c)):
                        sp.dma_start(a_rows[a:b, :], adj[c * P + a:c * P + b, :]).then_inc(a_loaded, 16)
                    with sp.Fori(0, HEADS) as d:
                        sp.wait_ge(top, HEADS * c + d + 1)
                        load_products(sp, qp_d, kp_d, d * N + c * P, rows_of(c), q, d * N, N, k_all, qk_loaded)

        @block.tensor
        def _(pe):
            flag = pe.value_load(over[0:1, 0:1], min_val=0, max_val=1)
            with pe.If(flag != 0):
                for c in range(C):
                    with pe.Fori(0, HEADS) as d:
                        pe.wait_ge(qk_loaded, LOADS * HEADS * c + LOADS * d + LOADS)
                        for a, b in col_pieces(N):
                            last = pe.matmul(py[:, a:b], q[:], k_all[:, a:b], start=True, stop=True)
                        last.then_inc(product, 1)
                    pe.wait_ge(top, HEADS * (c + 1) + 1)
                    pe.transpose(turn[:], tops[:], ident[:]).then_inc(turned, 1)

        @block.vector
        def _(dve):
            flag = dve.value_load(over[0:1, 0:1], min_val=0, max_val=1)
            with dve.If(flag != 0):
                dve.memset(q[:], 0.0).then_inc(zeroed, 1)
                dve.memset(k_all[:], 0.0).then_inc(zeroed, 1)
                dve.memset(tops[:], 0.0).then_inc(q_zero, 1)
                dve.wait_ge(q_zero, 1)
                dve.sem_inc(top, 1)
                for c in range(C):
                    r = rows_of(c)
                    dve.wait_ge(a_loaded, 16 * (c + 1) + (16 if c == C - 1 else 0))
                    with dve.Fori(0, HEADS) as d:
                        dve.wait_ge(product, HEADS * c + d + 1)
                        dve.scalar_tensor_tensor(out=scores[0:r, :], in0=a_rows[0:r, :], scalar=2.0, in1=py[0:r, 0:N],
                                                 op0=ALU.mult, op1=ALU.add).then_inc(added, 1)
                        dve.wait_ge(added, HEADS * c + d + 1)
                        dve.tensor_reduce(tops[0:r, bass.ds(d, 1)], scores[0:r, :], AX_X, ALU.max).then_inc(top, 1)
                        dve.wait_ge(top, HEADS * c + d + 2)
                    dve.wait_ge(turned, c + 1)
                    dve.tensor_copy(shift[:, c * P:(c + 1) * P], turn[:]).then_inc(kept, 1)
                    dve.wait_ge(kept, c + 1)


def load_products(sp, qp_d, kp_d, q_at, q_n, q_sb, k_at, k_n, k_sb, done):
    rows = PARTS * H
    for a in range(PARTS):
        sp.dma_start(k_sb[a * rows:(a + 1) * rows, 0:k_n], bass.AP(kp_d, k_at, [[TOK, rows], [1, k_n]])).then_inc(done, 16)
        for b in range(PARTS):
            at = (PARTS * a + b) * H
            sp.dma_start(q_sb[at:at + H, 0:q_n], bass.AP(qp_d, a * H * TOK + q_at, [[TOK, H], [1, q_n]])).then_inc(done, 16)


def split_shift(nc, shift, shift_d):
    with ExitStack() as ctx:
        s = Scope(nc, ctx, "sh")
        parts = [s.sb(f"part{k}", [P, N], BF16) for k in range(PARTS)]
        rest = [s.sb(f"rest{k}", [P, N]) for k in range(2)]
        steps, stored = s.sem("steps"), s.sem("stored")
        block = ctx.enter_context(nc.Block())

        @block.vector
        def _(dve):
            chain = Chain(dve, steps)
            dve.tensor_scalar(parts[0][:], shift[:, 0:N], -1.0, None, ALU.mult).then_inc(steps, 1)
            chain.done()
            dve.scalar_tensor_tensor(out=rest[0][:], in0=shift[:, 0:N], scalar=-1.0, in1=parts[0][:], op0=ALU.mult,
                                     op1=ALU.subtract).then_inc(steps, 1)
            chain.done()
            dve.tensor_copy(parts[1][:], rest[0][:]).then_inc(steps, 1)
            chain.done()
            dve.tensor_tensor(parts[2][:], rest[0][:], parts[1][:], ALU.subtract).then_inc(steps, 1)

        @block.sync
        def _(sp):
            sp.wait_ge(steps, 4)
            for k in range(PARTS):
                sp.dma_start(bass.AP(shift_d, k * HEADS * N, [[N, HEADS], [1, N]]), parts[k][:]).then_inc(stored, 16)
            sp.wait_ge(stored, 16 * PARTS)


def attend(nc, at_d, qp_d, kp_d, v_d, shift_d, o_d):
    with ExitStack() as ctx:
        s = Scope(nc, ctx, "at")
        at = s.sb("at", [P, C, NB])
        ring = [s.sb(f"ring{k}", [P, NB]) for k in range(RING)]
        q = [s.sb(f"q{k}", [P, NB], BF16) for k in range(PAIR)]
        k_all = [s.sb(f"k{k}", [P, NP], BF16) for k in range(PAIR)]
        v = [s.sb(f"v{k}", [P, C, VW]) for k in range(PAIR)]
        o = [s.sb(f"o{k}", [P, QW]) for k in range(PAIR)]
        score = [s.ps(f"score{k}", [P, 3 * BANK]) for k in range(2)]
        acc = [s.ps(f"acc{k}", [P, BANK]) for k in range(PAIR)]
        cleared, k_zero = s.sem("cleared"), s.sem("k_zero")
        at_loaded = s.sem("at_loaded")
        head_loaded = [s.sem(f"head_loaded{k}") for k in range(PAIR)]
        scored = s.sem("scored")
        added = s.sem("added")
        exped = s.sem("exped")
        used = s.sem("used")
        kept = s.sem("kept")
        stored = s.sem("stored")
        o_free = s.sem("o_free")
        block = ctx.enter_context(nc.Block())
        STEPS = PAIR * C
        HPB = HEADS // PAIR
        PAIRS = BLOCKS * HPB
        LOADS = 16 * (PARTS + PARTS * PARTS + 1 + 3)
        STORES = 16 * COLT
        CLEARED = 4 * PAIR
        assert STEPS % RING == 0 and STEPS % 2 == 0

        @block.sync
        def _(sp):
            sp.wait_ge(cleared, CLEARED)
            for b in range(BLOCKS):
                with sp.Fori(0, HPB) as i:
                    for k in range(PAIR):
                        d = PAIR * i + k
                        sp.wait_ge(used, (b * HEADS + d + 1) * C)
                        load_products(sp, qp_d, kp_d, d * N + b * NB, NB, q[k], d * N, N, k_all[k], head_loaded[k])
                        sp.dma_start(q[k][SHIFT_ROW:SHIFT_ROW + PARTS, :],
                                     bass.AP(shift_d, d * N + b * NB, [[HEADS * N, PARTS], [1, NB]])).then_inc(head_loaded[k], 16)
                        sp.dma_start(v[k][:, 0:C - 1, :].rearrange("p j w -> p (j w)"),
                                     bass.AP(v_d, d * (N * VW), [[C * VW, P], [1, (C - 1) * VW]])).then_inc(head_loaded[k], 16)
                        for x, y in row_pieces(LAST):
                            sp.dma_start(v[k][x:y, C - 1, :], bass.AP(v_d, d * (N * VW) + (x * C + C - 1) * VW,
                                                                      [[C * VW, y - x], [1, VW]])).then_inc(head_loaded[k], 16)

        @block.gpsimd
        def _(pool):
            pool.sem_inc(o_free, PAIR)
            for b in range(BLOCKS):
                if b:
                    pool.wait_ge(added, b * HPB * STEPS)
                pool.dma_start(at[:], bass.AP(at_d, b * NB, [[C * NP, P], [NP, C], [1, NB]])).then_inc(at_loaded, 16)
                with pool.Fori(0, HPB) as i:
                    for k in range(PAIR):
                        d = PAIR * i + k
                        pool.wait_ge(kept, b * HEADS + d + 1 + PAIR)
                        for t in range(COLT):
                            pool.dma_start(bass.AP(o_d, d * N + b * NB + t * QS, [[TOK, VW], [1, QS + (QW - QS) * (t == COLT - 1)]]),
                                           o[k][32 * t:32 * t + VW, 0:QS + (QW - QS) * (t == COLT - 1)]).then_inc(stored, 16)
                        pool.wait_ge(stored, (b * HEADS + d) * STORES + STORES)
                        pool.sem_inc(o_free, 1)

        @block.tensor
        def _(pe):
            pe.sem_inc(used, STEPS)

            def scores(n):
                k, j = divmod(n % STEPS, C)
                keys = k_all[k][:].rearrange("r (p j) -> r j p", j=C)[:, j, :]
                for a, b in col_pieces(NB):
                    last = pe.matmul(score[n % 2][:, a:b], keys, q[k][:, a:b], start=True, stop=True)
                last.then_inc(scored, 1)

            def values(n):
                k, j = divmod(n, C)
                for t in range(COLT):
                    last = pe.matmul(acc[k][32 * t:32 * t + VW, 0:QW], v[k][:, j, :], ring[n % RING][:, t * QS:t * QS + QW],
                                     start=(j == 0), stop=(j == C - 1), tile_position=(0, 32 * t))
                last.then_inc(used, 1)

            def pair(i, more):
                for n in range(STEPS):
                    if n + 2 < STEPS or more:
                        if n + 2 == STEPS:
                            pe.wait_ge(head_loaded[0], LOADS * i + 2 * LOADS)
                        if n + 2 == C:
                            pe.wait_ge(head_loaded[1], LOADS * i + LOADS)
                        pe.wait_ge(added, STEPS * i + n + 1)
                        scores(n + 2)
                    if n % C == 0:
                        pe.wait_ge(kept, PAIR * i + n // C + 1)
                    pe.wait_ge(exped, STEPS * i + n + 1)
                    values(n)

            pe.wait_ge(cleared, CLEARED)
            pe.wait_ge(head_loaded[0], LOADS)
            scores(0)
            scores(1)
            with pe.Fori(0, PAIRS - 1) as i:
                pair(i, True)
            pair(PAIRS - 1, False)

        @block.vector
        def _(dve):
            for k in range(PAIR):
                dve.memset(k_all[k][:], 0.0).then_inc(k_zero, 1)
                dve.memset(q[k][:], 0.0).then_inc(cleared, 1)
                dve.memset(v[k][:], 0.0).then_inc(cleared, 1)
                dve.memset(acc[k][:, 0:QW], 0.0).then_inc(cleared, 1)
            dve.wait_ge(k_zero, PAIR)
            for k in range(PAIR):
                dve.memset(k_all[k][SHIFT_ROW:SHIFT_ROW + PARTS, 0:N], 1.0).then_inc(cleared, 1)
            for b in range(BLOCKS):
                dve.wait_ge(at_loaded, 16 * b + 16)
                with dve.Fori(0, HPB) as i:
                    for n in range(STEPS):
                        done = STEPS * i + b * HPB * STEPS + n
                        dve.wait_ge(scored, done + 1)
                        dve.wait_ge(used, done + 1 - RING + STEPS)
                        dve.scalar_tensor_tensor(out=ring[n % RING][:], in0=at[:, n % C, :], scalar=2.0,
                                                 in1=score[n % 2][:, 0:NB], op0=ALU.mult, op1=ALU.add).then_inc(added, 1)

        @block.scalar
        def _(act):
            act.sem_inc(kept, PAIR)

            def keep_head(i, k):
                act.wait_ge(used, STEPS * i + (k + 1) * C + STEPS)
                act.wait_ge(o_free, PAIR * i + k + 1)
                act.activation(o[k][:], acc[k][:, 0:QW], ACT.Copy).then_inc(kept, 1)

            with act.Fori(0, PAIRS) as i:
                for n in range(STEPS):
                    act.wait_ge(added, STEPS * i + n + 1)
                    act.activation(ring[n % RING][:], ring[n % RING][:], ACT.Exp).then_inc(exped, 1)
                    if n == C + 2:
                        keep_head(i, 0)
                keep_head(i, 1)


def project_out(nc, o_d, out, keep):
    with ExitStack() as ctx:
        s = Scope(nc, ctx, "po")
        raw = [s.sb(f"raw{k}", [P, VW, P]) for k in range(2)]
        inv = s.sb("inv", [P, P])
        scaled = [s.sb(f"scaled{k}", [P, H, P]) for k in range(2)]
        turned = [s.sb(f"turned{k}", [P, H, P]) for k in range(2)]
        result = [s.sb(f"result{k}", [P, F]) for k in range(2)]
        tp = [s.ps(f"tp{k}", [P, H, P]) for k in range(2)]
        py = [s.ps(f"py{k}", [P, BANK]) for k in range(2)]
        loaded = [s.sem(f"loaded{k}") for k in range(2)]
        stored, result_free = s.sem("stored"), s.sem("result_free")
        cleared, inverted, divided, turned_ready, turned_kept, product, added = [
            s.sem(n) for n in ("cleared", "inverted", "divided", "turned_ready", "turned_kept", "product", "added")]
        block = ctx.enter_context(nc.Block())

        def rows_of(c):
            return LAST if isinstance(c, int) and c == C - 1 else P

        @block.sync
        def _(sp):
            def load(c, k):
                sp.wait_ge(divided, c + 1)
                for a, b in ([(0, P)] if rows_of(c) == P else row_pieces(LAST)):
                    sp.dma_start(raw[k][a:b, :, :], bass.AP(o_d, c * (P * P) + a * P, [[P, b - a], [TOK, VW], [1, P]])).then_inc(loaded[k], 16)

            sp.wait_ge(cleared, 2)
            with sp.Fori(0, C // 2 - 1) as i:
                for k in range(2):
                    load(2 * i + k, k)
            for c in (C - 2, C - 1):
                load(c, c % 2)

        @block.gpsimd
        def _(pool):
            def store(c, k):
                pool.wait_ge(added, c + 3)
                r = rows_of(c)
                pool.dma_start(bass.AP(out.tensor, c * (P * F), [[F, r], [1, F]]), result[k][0:r, :]).then_inc(stored, 16)
                pool.wait_ge(stored, 16 * c + 16)
                pool.sem_inc(result_free, 1)

            pool.sem_inc(result_free, 2)
            with pool.Fori(0, C // 2 - 1) as i:
                for k in range(2):
                    store(2 * i + k, k)
            for c in (C - 2, C - 1):
                store(c, c % 2)

        @block.tensor
        def _(pe):
            pe.sem_inc(turned_ready, 2)
            pe.sem_inc(product, 2)
            with pe.Fori(0, C // 2) as i:
                for k in range(2):
                    c = 2 * i + k
                    pe.wait_ge(divided, c + 3)
                    pe.wait_ge(turned_kept, c + 1)
                    for h in range(H):
                        last = pe.transpose(tp[k][:, h, :], scaled[k][:, h, :], keep["ident"][:])
                    last.then_inc(turned_ready, 1)
                    pe.wait_ge(turned_kept, c + 3)
                    pe.wait_ge(added, c + 1)
                    for h in range(H):
                        last = pe.matmul(py[k][:, 0:F], turned[k][:, h, :], keep["wo_t"][:, h, :], start=(h == 0), stop=(h == H - 1))
                    last.then_inc(product, 1)

        @block.scalar
        def _(act):
            act.sem_inc(turned_kept, 2)
            with act.Fori(0, C // 2) as i:
                for k in range(2):
                    c = 2 * i + k
                    act.wait_ge(turned_ready, c + 3)
                    act.wait_ge(product, c + 1)
                    act.activation(turned[k][:], tp[k][:], ACT.Copy).then_inc(turned_kept, 1)

        @block.vector
        def _(dve):
            dve.sem_inc(divided, 2)
            dve.sem_inc(added, 2)
            for k in range(2):
                dve.memset(raw[k][:], 1.0).then_inc(cleared, 1)

            def divide(c, k, count):
                dve.wait_ge(loaded[k], count)
                dve.wait_ge(divided, c + 2)
                dve.reciprocal(inv[:], raw[k][:, H, :]).then_inc(inverted, 1)
                dve.wait_ge(inverted, c + 1)
                dve.wait_ge(turned_ready, c + 1)
                dve.tensor_tensor(scaled[k][:], raw[k][:, 0:H, :], inv[:].unsqueeze(1).to_broadcast([P, H, P]),
                                  ALU.mult).then_inc(divided, 1)

            def add(c, k):
                dve.wait_ge(product, c + 3)
                dve.wait_ge(result_free, c + 1)
                dve.tensor_tensor(result[k][:], py[k][:, 0:F], keep["x"][:, c, :], ALU.add).then_inc(added, 1)

            with dve.Fori(0, C // 2 - 1) as i:
                for k in range(2):
                    divide(2 * i + k, k, 16 * i + 16)
                    add(2 * i + k, k)
            for c in (C - 2, C - 1):
                divide(c, c % 2, 16 * (c // 2) + 16 + (16 if c == C - 1 else 0))
                add(c, c % 2)


def gnn_two_layers(nc, x, adj, w_in, w_out, wq, wk, wv, wo, out):
    at_d = nc.dram_tensor("adj_t_scratch", (P, C, NP), F32)
    amax_d = nc.dram_tensor("amax_scratch", (NP,), F32)
    qp_d = nc.dram_tensor("q_parts_scratch", (PARTS, H, TOK), BF16)
    kp_d = nc.dram_tensor("k_parts_scratch", (PARTS, H, TOK), BF16)
    v_d = nc.dram_tensor("v_scratch", (TOK, VW), F32)
    nq_d = nc.dram_tensor("q_norm_scratch", (TOK,), F32)
    nk_d = nc.dram_tensor("k_norm_scratch", (TOK,), F32)
    shift_d = nc.dram_tensor("shift_scratch", (PARTS, HEADS, N), BF16)
    o_d = nc.dram_tensor("attended_scratch", (VW, TOK), F32)
    with ExitStack() as ctx:
        s = Scope(nc, ctx, "all")
        keep = {"x": s.sb("x", [P, C, F]), "ident": s.sb("ident", [P, P]), "ones": s.sb("ones", [P, 1]),
                "wo_t": s.sb("wo_t", [P, H, P])}
        with ExitStack() as early:
            e = Scope(nc, early, "early")
            keep |= {"h_nat": e.sb("h_nat", [P, C, F]), "w_t": e.sb("w_t", [P, 3 * H * P]), "h_t": e.sb("h_t", [P, NP])}
            with ExitStack() as layer:
                y = Scope(nc, layer, "layer1")
                keep |= {"h_int": y.sb("h_int", [P, C, F]), "in_acc": y.sb("in_acc", [P, NP]),
                         "out_acc": y.sb("out_acc", [P, NP]), "col_acc": y.sb("col_acc", [P, NP]),
                         "row_sum": y.sb("row_sum", [P, C])}
                load_and_norm_first(nc, x, keep)
                stream_adjacency(nc, adj, at_d, amax_d, keep)
                finish_first_layer(nc, w_in, w_out, wq, wk, wv, wo, keep)
            project(nc, qp_d, kp_d, v_d, nq_d, nk_d, keep)
        with ExitStack() as middle:
            m = Scope(nc, middle, "softmax")
            shift, over = m.sb("shift", [P, NP]), m.sb("over", [1, 1], I32)
            bound_scores(nc, nq_d, nk_d, amax_d, shift, over)
            take_true_maxima(nc, adj, qp_d, kp_d, shift, over, keep["ident"])
            split_shift(nc, shift, shift_d)
        attend(nc, at_d, qp_d, kp_d, v_d, shift_d, o_d)
        project_out(nc, o_d, out, keep)


_INS = ["x", "adj", "L0_gnn_W_in", "L0_gnn_W_out", "L1_gnn_Wq", "L1_gnn_Wk", "L1_gnn_Wv", "L1_gnn_Wo"]
_OUTS = [((N, F), "float32")]


def kernel(**inputs):
    import numpy as _np
    import concourse.bacc as _bacc
    from concourse import mybir as _mybir
    from concourse.bass_utils import run_bass_kernel_spmd as _run

    nc = _bacc.Bacc("TRN2", target_bir_lowering=False, num_devices=1)
    arrays, args = {}, []
    for name in _INS:
        a = _np.ascontiguousarray(inputs[name])
        arrays[f"in_{name}_dram"] = a
        args.append(nc.dram_tensor(f"in_{name}_dram", a.shape, _mybir.dt.from_np(a.dtype), kind="ExternalInput").ap())
    for i, (shape, dtype) in enumerate(_OUTS):
        dt = _mybir.dt.from_np(_np.dtype(dtype))
        args.append(nc.dram_tensor(f"out_{i}_dram", shape, dt, kind="ExternalOutput").ap())
    gnn_two_layers(nc, *args)
    r = _run(nc, [arrays], core_ids=[0])
    got = tuple(r.results[0][f"out_{i}_dram"] for i in range(len(_OUTS)))
    return got[0]
```

```python
from contextlib import ExitStack

import concourse.bass as bass
from concourse import mybir

ALU = mybir.AluOpType
ACT = mybir.ActivationFunctionType
F32 = mybir.dt.float32
BF16 = mybir.dt.bfloat16
I32 = mybir.dt.int32
AX_X = mybir.AxisListType.X

P = 128
N = 3327
F = 128
H = 8
HEADS = 128
C = -(-N // P)
NP = C * P
LAST = N - (C - 1) * P
TOK = NP * P
BANK = 512
EPS = 1e-5
SCALE = float(F) ** -0.5

BLOCKS = 4
NB = -(-N // BLOCKS)
assert N <= NB * BLOCKS <= NP
SCORES = 3
PARTS = 3
PROD = PARTS * PARTS * H
SHIFT_ROW = 96
VW = H + 1
COLT = 4
QW = NB // COLT
assert QW * COLT == NB
DOUBLES = 8
SINGLES = 4
GROUP = 4
CHUNKS_AT_ONCE = 5
PRODUCTS = 6
LIMIT = 30.0


def row_pieces(total):
    whole = total // 16 * 16
    return [(0, whole)] + ([(whole, total)] if total > whole else [])


def col_pieces(width):
    return [(a, min(a + BANK, width)) for a in range(0, width, BANK)]


def normalise(dve, x, h, centred, stats, chain, rooted, variance_ready, root_count):
    step = chain
    dve.tensor_reduce(stats[:, 0, :], x, AX_X, ALU.add).then_inc(step.sem, 1)
    step.done()
    dve.tensor_scalar(stats[:, 0, :], stats[:, 0, :], 1.0 / F, None, ALU.mult).then_inc(step.sem, 1)
    step.done()
    for c in range(C):
        last = dve.tensor_scalar(centred[:, c, :], x[:, c, :], stats[:, 0, c:c + 1], None, ALU.subtract)
    last.then_inc(step.sem, 1)
    step.done()
    dve.tensor_tensor(h, centred[:], centred[:], ALU.mult).then_inc(step.sem, 1)
    step.done()
    dve.tensor_reduce(stats[:, 1, :], h, AX_X, ALU.add).then_inc(step.sem, 1)
    step.done()
    dve.tensor_scalar(stats[:, 1, :], stats[:, 1, :], 1.0 / F, EPS, ALU.mult, ALU.add).then_inc(variance_ready, 1)
    dve.wait_ge(rooted, root_count)
    dve.reciprocal(stats[:, 3, :], stats[:, 2, :]).then_inc(step.sem, 1)
    step.done()
    for c in range(C):
        last = dve.tensor_scalar(h[:, c, :], centred[:, c, :], stats[:, 3, c:c + 1], 0.0, ALU.mult, ALU.max)
    last.then_inc(step.sem, 1)
    step.done()


class Chain:

    def __init__(self, engine, sem):
        self.engine, self.sem, self.count = engine, sem, 0

    def done(self):
        self.count += 1
        self.engine.wait_ge(self.sem, self.count)


class Scope:

    def __init__(self, nc, ctx, tag):
        self.nc, self.ctx, self.tag = nc, ctx, tag

    def sb(self, name, shape, dt=F32):
        return self.ctx.enter_context(self.nc.sbuf_tensor(f"{self.tag}_{name}", shape, dt))

    def ps(self, name, shape, dt=F32):
        return self.ctx.enter_context(self.nc.psum_tensor(f"{self.tag}_{name}", shape, dt))

    def sem(self, name):
        return self.ctx.enter_context(self.nc.semaphore(f"{self.tag}_{name}"))


def load_and_norm_first(nc, x, keep):
    with ExitStack() as ctx:
        s = Scope(nc, ctx, "n1")
        x_int = s.sb("x_int", [P, C, F])
        centred = s.sb("centred", [P, C, F])
        stats = s.sb("stats", [P, 4, C])
        cleared, x_loaded = s.sem("cleared"), s.sem("x_loaded")
        variance_ready, rooted, steps = s.sem("variance_ready"), s.sem("rooted"), s.sem("steps")
        ident_zero, ident_done = s.sem("ident_zero"), s.sem("ident_done")
        x_nat = keep["x"]
        block = ctx.enter_context(nc.Block())
        loads = 1 + 2 * len(row_pieces(LAST)) + 1

        @block.sync
        def _(sp):
            sp.wait_ge(cleared, 2)
            sp.dma_start(x_nat[:, 0:C - 1, :], x[0:(C - 1) * P, :].rearrange("(c p) f -> p c f", p=P)).then_inc(x_loaded, 16)
            for a, b in row_pieces(LAST):
                sp.dma_start(x_nat[a:b, C - 1, :], x[(C - 1) * P + a:(C - 1) * P + b, :]).then_inc(x_loaded, 16)
                sp.dma_start(x_int[a:b, :, :], x[C * a:C * b, :].rearrange("(p j) f -> p j f", j=C)).then_inc(x_loaded, 16)
            sp.dma_start(x_int[P - 1:P, 0:C - 1, :],
                         x[C * (P - 1):N, :].rearrange("(p j) f -> p j f", p=1)).then_inc(x_loaded, 16)

        @block.gpsimd
        def _(pool):
            pool.memset(keep["ident"][:], 0.0).then_inc(ident_zero, 1)
            pool.wait_ge(ident_zero, 1)
            pool.affine_select(out=keep["ident"][:], in_=keep["ident"][:], compare_op=ALU.not_equal, fill=1.0,
                               base=0, pattern=[[-1, P]], channel_multiplier=1).then_inc(ident_done, 1)

        @block.scalar
        def _(act):
            for k in range(2):
                act.wait_ge(variance_ready, k + 1)
                act.activation(stats[:, 2, :], stats[:, 1, :], ACT.Sqrt).then_inc(rooted, 1)

        @block.vector
        def _(dve):
            dve.memset(keep["ones"][:], 1.0)
            dve.memset(x_nat[:, C - 1, :], 0.0).then_inc(cleared, 1)
            dve.memset(x_int[:, C - 1, :], 0.0).then_inc(cleared, 1)
            dve.wait_ge(x_loaded, 16 * loads)
            chain = Chain(dve, steps)
            normalise(dve, x_nat[:], keep["h_nat"][:], centred, stats, chain, rooted, variance_ready, 1)
            normalise(dve, x_int[:], keep["h_int"][:], centred, stats, chain, rooted, variance_ready, 2)


def stream_adjacency(nc, adj, at_d, et_d, amax_d, keep):
    with ExitStack() as ctx:
        s = Scope(nc, ctx, "st")
        a_rows = [s.sb(f"a_rows{k}", [P, NP]) for k in range(2)]
        a_t = [s.sb(f"a_t{k}", [P, C, P]) for k in range(2)]
        e_t = [s.sb(f"e_t{k}", [P, PRODUCTS, P]) for k in range(2)]
        h_now = [s.sb(f"h_now{k}", [P, F]) for k in range(2)]
        zero_row = s.sb("zero_row", [1, NP])
        row_max = s.sb("row_max", [P, C])
        tp = [s.ps(f"tp{k}", [P, BANK]) for k in range(2)]
        out_sum = [s.ps(f"out_sum{k}", [P, BANK]) for k in range(2)]
        in_sum = [s.ps(f"in_sum{k}", [P, BANK]) for k in range(2)]
        cleared = s.sem("cleared")
        a_loaded = [s.sem(f"a_loaded{k}") for k in range(2)]
        last_loaded, max_stored = s.sem("last_loaded"), s.sem("max_stored")
        h_copied, at_copied = s.sem("h_copied"), s.sem("at_copied")
        at_stored = [s.sem(f"at_stored{k}") for k in range(2)]
        transposed, out_ready, out_added = s.sem("transposed"), s.sem("out_ready"), s.sem("out_added")
        in_ready, in_copied = s.sem("in_ready"), s.sem("in_copied")
        dve_read, pool_added, out_zero = s.sem("dve_read"), s.sem("pool_added"), s.sem("out_zero")
        block = ctx.enter_context(nc.Block())
        groups = [range(g, min(g + 4, C)) for g in range(0, C, 4)]
        G = len(groups)
        pieces = col_pieces(NP)
        assert len(pieces) == G
        FREE = 2

        @block.sync
        def _(sp):
            def load(c, k):
                sp.dma_start(a_rows[k][:, 0:N], bass.AP(adj.tensor, c * (P * N), [[N, P], [1, N]])).then_inc(a_loaded[k], 16)

            def store(c, k):
                sp.wait_ge(at_copied, G * c + G + FREE)
                sp.dma_start(bass.AP(at_d, c * P, [[C * NP, P], [NP, C], [1, P]]), a_t[k][:]).then_inc(at_stored[k], 16)
                sp.dma_start(bass.AP(et_d, c * P, [[PRODUCTS * NP, P], [NP, PRODUCTS], [1, P]]), e_t[k][:]).then_inc(at_stored[k], 16)

            def all_read(c):
                sp.wait_ge(in_ready, c + 1 + FREE)
                sp.wait_ge(dve_read, c + 1 + FREE)
                sp.wait_ge(pool_added, c + 1 + FREE)

            for k in range(2):
                sp.sem_inc(at_stored[k], 32)
            sp.wait_ge(cleared, 3)
            load(0, 0)
            load(1, 1)
            with sp.Fori(0, C // 2 - 2) as i:
                for k in range(2):
                    store(2 * i + k, k)
                    all_read(2 * i + k)
                    load(2 * i + k + 2, k)
            store(C - 4, 0)
            all_read(C - 4)
            load(C - 2, 0)
            store(C - 3, 1)
            all_read(C - 3)
            (_, whole), (_, rest) = row_pieces(LAST)
            sp.dma_start(a_rows[1][LAST:P, :], zero_row[:]).then_inc(last_loaded, 16)
            sp.dma_start(a_rows[1][whole:rest, 0:N], adj[(C - 1) * P + whole:N, :]).then_inc(last_loaded, 16)
            sp.wait_ge(last_loaded, 32)
            sp.dma_start(a_rows[1][0:whole, 0:N], adj[(C - 1) * P:(C - 1) * P + whole, :]).then_inc(a_loaded[1], 16)
            store(C - 2, 0)
            store(C - 1, 1)
            sp.wait_ge(dve_read, C + FREE)
            sp.dma_start(bass.AP(amax_d, 0, [[1, P], [P, C], [1, 1]]), row_max[:].rearrange("p (c o) -> p c o", o=1),
                         allow_slow_non_contiguous=True).then_inc(max_stored, 16)
            sp.wait_ge(max_stored, 16)
            for k in range(2):
                sp.wait_ge(at_stored[k], 32 * (C // 2) + 32)

        @block.gpsimd
        def _(pool):
            pool.memset(zero_row[:], 0.0).then_inc(cleared, 1)
            pool.memset(keep["col_acc"][:], 0.0).then_inc(pool_added, FREE)
            with pool.Fori(0, C // 2) as i:
                for k in range(2):
                    c = 2 * i + k
                    pool.wait_ge(in_ready, c + 1)
                    pool.tensor_copy(h_now[k][:], keep["h_nat"][:, c, :]).then_inc(h_copied, 1)
                    pool.wait_ge(a_loaded[k], 16 * i + 16)
                    pool.wait_ge(pool_added, c + FREE)
                    pool.tensor_tensor(keep["col_acc"][:], keep["col_acc"][:], a_rows[k][:], ALU.add).then_inc(pool_added, 1)

        @block.tensor
        def _(pe):
            pe.sem_inc(in_ready, FREE)
            with pe.Fori(0, C // 2) as i:
                for k in range(2):
                    c = 2 * i + k
                    a_cols = a_rows[k][:].rearrange("p (q j) -> p j q", j=C)
                    pe.wait_ge(a_loaded[k], 16 * i + 16)
                    pe.wait_ge(h_copied, c + 1)
                    for g in range(G + 1):
                        if g < G:
                            pe.wait_ge(at_copied, G * c + g + 1)
                            for m, j in enumerate(groups[g]):
                                last = pe.transpose(tp[(G * k + g) % 2][:, m * P:(m + 1) * P], a_cols[:, j, :], keep["ident"][:])
                            last.then_inc(transposed, 1)
                            a, b = pieces[g]
                            pe.wait_ge(out_added, G * c + g + 1)
                            pe.matmul(out_sum[(G * k + g) % 2][:, 0:b - a], h_now[k][:], a_rows[k][:, a:b],
                                      start=True, stop=True).then_inc(out_ready, 1)
                        if g == 0:
                            continue
                        if g == 1:
                            pe.wait_ge(in_copied, c + 1)
                        pe.wait_ge(at_copied, G * c + g + FREE)
                        for j in groups[g - 1]:
                            last = pe.matmul(in_sum[k][:, 0:P], keep["h_int"][:, j, :], a_t[k][:, j, :],
                                             start=(j == 0), stop=(j == C - 1))
                    last.then_inc(in_ready, 1)

        @block.scalar
        def _(act):
            act.sem_inc(at_copied, FREE)
            act.sem_inc(in_copied, FREE)
            with act.Fori(0, C // 2) as i:
                for k in range(2):
                    c = 2 * i + k
                    act.wait_ge(in_ready, c + 1)
                    act.wait_ge(at_stored[k], 32 * i + 32)
                    for g in range(G):
                        j0, n = groups[g][0], len(groups[g])
                        act.wait_ge(transposed, G * c + g + 1)
                        e0 = max(j0, C - PRODUCTS)
                        if e0 < j0 + n:
                            act.activation(e_t[k][:, e0 - (C - PRODUCTS):j0 + n - (C - PRODUCTS), :].rearrange("p j n -> p (j n)"),
                                           tp[(G * k + g) % 2][:, (e0 - j0) * P:n * P], ACT.Exp, scale=2.0)
                        act.activation(a_t[k][:, j0:j0 + n, :].rearrange("p j n -> p (j n)"), tp[(G * k + g) % 2][:, 0:n * P],
                                       ACT.Copy).then_inc(at_copied, 1)
                    act.wait_ge(in_ready, c + 1 + FREE)
                    act.activation(keep["in_acc"][:, bass.ds(c * P, P)], in_sum[k][:, 0:P], ACT.Copy).then_inc(in_copied, 1)

        @block.vector
        def _(dve):
            dve.sem_inc(out_added, FREE)
            dve.sem_inc(dve_read, FREE)
            for k in range(2):
                dve.memset(a_rows[k][:, N:NP], 0.0).then_inc(cleared, 1)
            dve.memset(keep["out_acc"][:], 0.0).then_inc(out_zero, 1)
            dve.wait_ge(out_zero, 1)
            with dve.Fori(0, C // 2) as i:
                for k in range(2):
                    c = 2 * i + k
                    dve.wait_ge(a_loaded[k], 16 * i + 16)
                    for g in range(G):
                        a, b = pieces[g]
                        dve.wait_ge(out_ready, G * c + g + 1)
                        dve.wait_ge(out_added, G * c + g + 1)
                        dve.tensor_tensor(keep["out_acc"][:, a:b], keep["out_acc"][:, a:b],
                                          out_sum[(G * k + g) % 2][:, 0:b - a], ALU.add).then_inc(out_added, 1)
                        if g == 1:
                            dve.tensor_reduce(keep["row_sum"][:, bass.ds(c, 1)], a_rows[k][:], AX_X, ALU.add)
                        if g == 4:
                            dve.tensor_reduce(row_max[:, bass.ds(c, 1)], a_rows[k][:], AX_X, ALU.max,
                                              apply_absolute_value=True).then_inc(dve_read, 1)


def finish_first_layer(nc, w_in, w_out, wq, wk, wv, wo, keep):
    with ExitStack() as ctx:
        s = Scope(nc, ctx, "fl")
        mix = s.sb("mix", [P, 2, F])
        w_nat = s.sb("w_nat", [P, 3, H, F])
        wo_nat = s.sb("wo_nat", [P, H * P])
        centred = s.sb("centred", [P, C, F])
        stats = s.sb("stats", [P, 4, C])
        degree = s.sb("degree", [P, 4, 2, C])
        y = s.ps("y", [P, 8 * BANK])
        deg = y[:, 7 * BANK:7 * BANK + C]
        loaded, deg_ready, rdeg_ready = s.sem("loaded"), s.sem("deg_ready"), s.sem("rdeg_ready")
        mixed, x_ready, steps = s.sem("mixed"), s.sem("x_ready"), s.sem("steps")
        variance_ready, rooted = s.sem("variance_ready"), s.sem("rooted")
        h_ready, h_turned, h_kept, w_turned = s.sem("h_ready"), s.sem("h_turned"), s.sem("h_kept"), s.sem("w_turned")
        block = ctx.enter_context(nc.Block())
        x1, ident = keep["x"], keep["ident"]

        @block.sync
        def _(sp):
            sp.dma_start(mix[:, 0, :], w_in).then_inc(loaded, 16)
            sp.dma_start(mix[:, 1, :], w_out).then_inc(loaded, 16)
            for k, w in enumerate((wq, wk, wv)):
                sp.dma_start(w_nat[:, k, :, :], w.rearrange("(t h) f -> t h f", h=H)).then_inc(loaded, 16)
            sp.dma_start(wo_nat[:], wo).then_inc(loaded, 16)

        @block.tensor
        def _(pe):
            for c in range(C):
                last = pe.matmul(deg[:, c:c + 1], keep["col_acc"][:, c * P:(c + 1) * P], keep["ones"][:, 0:1],
                                 start=True, stop=True)
            last.then_inc(deg_ready, 1)
            pe.wait_ge(loaded, 16 * 6)
            for k, acc in enumerate((keep["in_acc"], keep["out_acc"])):
                if k:
                    pe.wait_ge(x_ready, 1)
                for c in range(C):
                    last = pe.matmul(y[:, c * P:(c + 1) * P], acc[:, c * P:(c + 1) * P], mix[:, k, :], start=True, stop=True)
                last.then_inc(mixed, 1)
            pe.wait_ge(h_ready, 1)
            for c in range(C):
                last = pe.transpose(y[:, c * P:(c + 1) * P], keep["h_nat"][:, c, :], ident[:])
            last.then_inc(h_turned, 1)
            pe.wait_ge(h_kept, 2)
            for k in range(3):
                for h in range(H):
                    at = (k * H + h) * P
                    last = pe.transpose(y[:, at:at + P], w_nat[:, k, h, :], ident[:])
            wo_cols = wo_nat[:].rearrange("o (t h) -> o h t", h=H)
            for h in range(H):
                at = (3 * H + h) * P
                last = pe.transpose(y[:, at:at + P], wo_cols[:, h, :], ident[:])
            last.then_inc(w_turned, 1)

        @block.scalar
        def _(act):
            act.wait_ge(variance_ready, 1)
            act.activation(stats[:, 2, :], stats[:, 1, :], ACT.Sqrt).then_inc(rooted, 1)
            act.wait_ge(h_turned, 1)
            act.activation(keep["h_t"][:, 4 * BANK:NP], y[:, 4 * BANK:NP], ACT.Copy).then_inc(h_kept, 1)
            act.wait_ge(w_turned, 1)
            act.activation(keep["w_t"][:, 4 * BANK:], y[:, 4 * BANK:6 * BANK], ACT.Copy)
            act.activation(keep["wo_t"][:].rearrange("p h o -> p (h o)"), y[:, 6 * BANK:8 * BANK], ACT.Copy)

        @block.vector
        def _(dve):
            chain = Chain(dve, steps)
            dve.tensor_copy(degree[:, 0, 0, :], keep["row_sum"][:])
            dve.wait_ge(deg_ready, 1)
            dve.tensor_copy(degree[:, 0, 1, :], deg).then_inc(steps, 1)
            chain.done()
            dve.tensor_scalar(degree[:, 1, :, :], degree[:, 0, :, :], 0.0, None, ALU.is_gt).then_inc(steps, 1)
            chain.done()
            dve.tensor_tensor(degree[:, 2, :, :], degree[:, 0, :, :], degree[:, 1, :, :], ALU.mult)
            dve.tensor_scalar(degree[:, 3, :, :], degree[:, 1, :, :], -1.0, 1.0, ALU.mult, ALU.add).then_inc(steps, 1)
            chain.done()
            dve.tensor_tensor(degree[:, 0, :, :], degree[:, 2, :, :], degree[:, 3, :, :], ALU.add).then_inc(steps, 1)
            chain.done()
            dve.reciprocal(degree[:, 1, :, :], degree[:, 0, :, :]).then_inc(steps, 1)
            chain.done()
            for k in range(2):
                dve.wait_ge(mixed, k + 1)
                for c in range(C):
                    last = dve.scalar_tensor_tensor(out=x1[:, c, :], in0=y[:, c * P:(c + 1) * P], scalar=degree[:, 1, k, c:c + 1],
                                                    in1=x1[:, c, :], op0=ALU.mult, op1=ALU.add)
                last.then_inc(x_ready, 1)
                dve.wait_ge(x_ready, k + 1)
            normalise(dve, x1[:], keep["h_nat"][:], centred, stats, chain, rooted, variance_ready, 1)
            dve.sem_inc(h_ready, 1)
            dve.wait_ge(h_turned, 1)
            dve.tensor_copy(keep["h_t"][:, 0:4 * BANK], y[:, 0:4 * BANK]).then_inc(h_kept, 1)
            dve.wait_ge(w_turned, 1)
            dve.tensor_copy(keep["w_t"][:, 0:4 * BANK], y[:, 0:4 * BANK])


def project(nc, qp_d, kp_d, v_d, nq_d, nk_d, keep):
    with ExitStack() as ctx:
        s = Scope(nc, ctx, "pr")
        W = H * P
        parts = [[s.sb(f"parts{kind}{k}", [P, PARTS, W], BF16) for kind in "qk"] for k in range(2)]
        rest = [s.sb(f"rest{kind}", [P, W]) for kind in "qk"]
        squares = [s.sb(f"squares{kind}", [P, W]) for kind in "qk"]
        value = [s.sb(f"value{k}", [P, P, VW]) for k in range(2)]
        norm2 = [s.sb(f"norm2{kind}", [P, C, P]) for kind in "qk"]
        h_now = [s.sb(f"h_now{k}", [P, P]) for k in range(2)]
        py = [s.ps(f"py{kind}", [P, W]) for kind in "qkv"]
        h_copied, product = s.sem("h_copied"), [s.sem(f"product_{kind}") for kind in "qkv"]
        rest_left, part2, part3 = [[s.sem(f"{n}_{kind}") for kind in "qk"] for n in ("rest_left", "part2", "part3")]
        squared, summed = [[s.sem(f"{n}_{kind}") for kind in "qk"] for n in ("squared", "summed")]
        value_kept, ones_set, rooted, norm_stored = s.sem("value_kept"), s.sem("ones_set"), s.sem("rooted"), s.sem("norm_stored")
        parts_stored = [[s.sem(f"parts_stored{k}{kind}") for kind in "qk"] for k in range(2)]
        value_stored = [s.sem(f"value_stored{k}") for k in range(2)]
        block = ctx.enter_context(nc.Block())
        PS = 16 * PARTS

        @block.sync
        def _(sp):
            for k in range(2):
                for kind in range(2):
                    sp.sem_inc(parts_stored[k][kind], PS)
                sp.sem_inc(value_stored[k], 16)
            with sp.Fori(0, C // 2) as i:
                for k in range(2):
                    c = 2 * i + k
                    for kind, dst in enumerate((qp_d, kp_d)):
                        sp.wait_ge(part3[kind], c + 2)
                        for part in range(PARTS):
                            sp.dma_start(bass.AP(dst, part * H * TOK + c * (P * P), [[P, P], [TOK, H], [1, P]]),
                                         parts[k][kind][:, part, :].rearrange("p (h t) -> p h t", h=H)).then_inc(parts_stored[k][kind], 16)
                    sp.wait_ge(value_kept, c + 2)
                    sp.dma_start(bass.AP(v_d, c * (P * P * VW), [[P * VW, P], [1, P * VW]]),
                                 value[k][:].rearrange("p t v -> p (t v)")).then_inc(value_stored[k], 16)
            sp.wait_ge(rooted, 2)
            for kind, dst in enumerate((nq_d, nk_d)):
                sp.dma_start(bass.AP(dst, 0, [[P, P], [P * P, C], [1, P]]), norm2[kind][:]).then_inc(norm_stored, 16)
            sp.wait_ge(norm_stored, 32)
            for k in range(2):
                for kind in range(2):
                    sp.wait_ge(parts_stored[k][kind], PS * (C // 2) + PS)
                sp.wait_ge(value_stored[k], 16 * (C // 2) + 16)

        @block.gpsimd
        def _(pool):
            for kind in range(2):
                pool.sem_inc(part3[kind], 1)
            def copy_h(c, k):
                pool.wait_ge(product[2], c + 1)
                pool.tensor_copy(h_now[k][:], keep["h_t"][:, bass.ds(c * P, P)]).then_inc(h_copied, 1)

            def body(i, more):
                for k in range(2):
                    c = 2 * i + k
                    if k == 0 or more:
                        copy_h(c + 1, 1 - k)
                    for kind in range(2):
                        pool.wait_ge(part2[kind], c + 1)
                        pool.tensor_tensor(parts[k][kind][:, 2, :], rest[kind][:], parts[k][kind][:, 1, :],
                                           ALU.subtract).then_inc(part3[kind], 1)

            copy_h(0, 0)
            with pool.Fori(0, C // 2 - 1) as i:
                body(i, True)
            body(C // 2 - 1, False)

        @block.tensor
        def _(pe):
            pe.sem_inc(product[2], 2)
            with pe.Fori(0, C // 2) as i:
                for k in range(2):
                    c = 2 * i + k
                    pe.wait_ge(h_copied, c + 1)
                    for kind in range(3):
                        if kind < 2:
                            pe.wait_ge(rest_left[kind], c + 1)
                            pe.wait_ge(squared[kind], c + 1)
                        else:
                            pe.wait_ge(value_kept, c + 1)
                        for b in range(0, W, BANK):
                            last = pe.matmul(py[kind][:, b:b + BANK], h_now[k][:], keep["w_t"][:, kind * W + b:kind * W + b + BANK],
                                             start=True, stop=True)
                        last.then_inc(product[kind], 1)

        @block.scalar
        def _(act):
            for kind in range(2):
                act.sem_inc(squared[kind], 1)
            act.sem_inc(value_kept, 1)
            act.wait_ge(ones_set, 2)
            with act.Fori(0, C // 2) as i:
                for k in range(2):
                    c = 2 * i + k
                    for kind in range(2):
                        act.wait_ge(parts_stored[k][kind], PS * i + PS)
                        act.wait_ge(product[kind], c + 1)
                        act.activation(parts[k][kind][:, 0, :], py[kind][:], ACT.Copy, scale=(SCALE, 1.0)[kind])
                        act.wait_ge(summed[kind], c + 1)
                        act.activation(squares[kind][:], py[kind][:], ACT.Square).then_inc(squared[kind], 1)
                    for kind in range(2):
                        act.wait_ge(rest_left[kind], c + 2)
                        act.activation(parts[k][kind][:, 1, :], rest[kind][:], ACT.Copy).then_inc(part2[kind], 1)
                    act.wait_ge(product[2], c + 3)
                    act.wait_ge(value_stored[k], 16 * i + 16)
                    act.activation(value[k][:, :, 0:H].rearrange("p t h -> p h t"),
                                   py[2][:].rearrange("p (h t) -> p h t", h=H), ACT.Copy).then_inc(value_kept, 1)
            for kind in range(2):
                act.wait_ge(summed[kind], C + 1)
                act.activation(norm2[kind][:], norm2[kind][:], ACT.Sqrt, scale=(SCALE * SCALE, 1.0)[kind]).then_inc(rooted, 1)

        @block.vector
        def _(dve):
            for k in range(2):
                dve.memset(value[k][:], 1.0).then_inc(ones_set, 1)
            for kind in range(2):
                dve.sem_inc(rest_left[kind], 1)
                dve.sem_inc(summed[kind], 1)
            with dve.Fori(0, C // 2) as i:
                for k in range(2):
                    c = 2 * i + k
                    for kind in range(2):
                        dve.wait_ge(squared[kind], c + 2)
                        dve.wait_ge(part3[kind], c + 1)
                        dve.scalar_tensor_tensor(out=rest[kind][:], in0=py[kind][:], scalar=(SCALE, 1.0)[kind],
                                                 in1=parts[k][kind][:, 0, :], op0=ALU.mult,
                                                 op1=ALU.subtract).then_inc(rest_left[kind], 1)
                        dve.tensor_reduce(norm2[kind][:, c, :], squares[kind][:].rearrange("p (h t) -> p t h", h=H),
                                          AX_X, ALU.add).then_inc(summed[kind], 1)


def bound_scores(nc, nq_d, nk_d, amax_d, shift, over):
    with ExitStack() as ctx:
        s = Scope(nc, ctx, "bo")
        nq, nk, amax = s.sb("nq", [P, N]), s.sb("nk", [P, N]), s.sb("amax", [P, N])
        small, turned = s.sb("small", [P, 2]), s.sb("turned", [1, P + 2])
        loaded, steps, top_ready, top_turned, top_stored = [s.sem(n) for n in ("loaded", "steps", "top_ready", "top_turned", "top_stored")]
        top_d = nc.dram_tensor("top_scratch", (P,), F32)
        block = ctx.enter_context(nc.Block())

        @block.sync
        def _(sp):
            for dst, src, step in ((nq, nq_d, N), (nk, nk_d, N), (amax, amax_d, 0)):
                sp.dma_start(dst[:], bass.AP(src, 0, [[step, HEADS], [1, N]])).then_inc(loaded, 16)
            sp.wait_ge(top_ready, 1)
            sp.dma_start(bass.AP(top_d, 0, [[1, P], [1, 1]]), small[:, 1:2]).then_inc(top_stored, 16)
            sp.wait_ge(top_stored, 16)
            sp.dma_start(turned[:, 0:P], bass.AP(top_d, 0, [[P, 1], [1, P]])).then_inc(top_turned, 16)

        @block.vector
        def _(dve):
            chain = Chain(dve, steps)
            dve.wait_ge(loaded, 48)
            dve.memset(shift[:, N:NP], 0.0)
            dve.tensor_reduce(small[:, 0:1], nk[:], AX_X, ALU.max)
            dve.tensor_scalar(amax[:], amax[:], 2.0, None, ALU.mult).then_inc(steps, 1)
            chain.done()
            dve.scalar_tensor_tensor(out=shift[:, 0:N], in0=nq[:], scalar=small[:, 0:1], in1=amax[:], op0=ALU.mult,
                                     op1=ALU.add).then_inc(steps, 1)
            chain.done()
            dve.tensor_reduce(small[:, 1:2], shift[:, 0:N], AX_X, ALU.max).then_inc(top_ready, 1)
            dve.wait_ge(top_turned, 16)
            dve.tensor_reduce(turned[:, P:P + 1], turned[:, 0:P], AX_X, ALU.max).then_inc(steps, 1)
            chain.done()
            dve.tensor_scalar(turned[:, P + 1:P + 2], turned[:, P:P + 1], LIMIT, None, ALU.is_gt).then_inc(steps, 1)
            chain.done()
            dve.tensor_copy(over[:], turned[:, P + 1:P + 2])


def take_true_maxima(nc, adj, qp_d, kp_d, shift, over, ident):
    with ExitStack() as ctx:
        s = Scope(nc, ctx, "mx")
        a_rows = s.sb("a_rows", [P, N])
        q = s.sb("q", [P, P], BF16)
        k_all = s.sb("k_all", [P, N], BF16)
        scores = s.sb("scores", [P, N])
        tops = s.sb("tops", [P, HEADS])
        py = s.ps("py", [P, 7 * BANK])
        turn = s.ps("turn", [P, P])
        q_now = s.sb("q_now", [P, P], BF16)
        a_loaded, qk_loaded, product, added, top = [s.sem(n) for n in ("a_loaded", "qk_loaded", "product", "added", "top")]
        turned, kept, zeroed, q_zero = s.sem("turned"), s.sem("kept"), s.sem("zeroed"), s.sem("q_zero")
        block = ctx.enter_context(nc.Block())
        LOADS = 16 * (3 + 9)

        def rows_of(c):
            return P if c < C - 1 else LAST

        @block.sync
        def _(sp):
            flag = sp.value_load(over[0:1, 0:1], min_val=0, max_val=1)
            with sp.If(flag != 0):
                sp.wait_ge(zeroed, 2)
                for c in range(C):
                    if c:
                        sp.wait_ge(kept, c)
                    for a, b in row_pieces(rows_of(c)):
                        sp.dma_start(a_rows[a:b, :], adj[c * P + a:c * P + b, :]).then_inc(a_loaded, 16)
                    with sp.Fori(0, HEADS) as d:
                        sp.wait_ge(top, HEADS * c + d + 1)
                        load_products(sp, qp_d, kp_d, d * N + c * P, rows_of(c), q, d * N, N, k_all, qk_loaded)

        @block.tensor
        def _(pe):
            flag = pe.value_load(over[0:1, 0:1], min_val=0, max_val=1)
            with pe.If(flag != 0):
                for c in range(C):
                    with pe.Fori(0, HEADS) as d:
                        pe.wait_ge(qk_loaded, LOADS * HEADS * c + LOADS * d + LOADS)
                        for a, b in col_pieces(N):
                            last = pe.matmul(py[:, a:b], q[:], k_all[:, a:b], start=True, stop=True)
                        last.then_inc(product, 1)
                    pe.wait_ge(top, HEADS * (c + 1) + 1)
                    pe.transpose(turn[:], tops[:], ident[:]).then_inc(turned, 1)

        @block.vector
        def _(dve):
            flag = dve.value_load(over[0:1, 0:1], min_val=0, max_val=1)
            with dve.If(flag != 0):
                dve.memset(q[:], 0.0).then_inc(zeroed, 1)
                dve.memset(k_all[:], 0.0).then_inc(zeroed, 1)
                dve.memset(tops[:], 0.0).then_inc(q_zero, 1)
                dve.wait_ge(q_zero, 1)
                dve.sem_inc(top, 1)
                for c in range(C):
                    r = rows_of(c)
                    dve.wait_ge(a_loaded, 16 * (c + 1) + (16 if c == C - 1 else 0))
                    with dve.Fori(0, HEADS) as d:
                        dve.wait_ge(product, HEADS * c + d + 1)
                        dve.scalar_tensor_tensor(out=scores[0:r, :], in0=a_rows[0:r, :], scalar=2.0, in1=py[0:r, 0:N],
                                                 op0=ALU.mult, op1=ALU.add).then_inc(added, 1)
                        dve.wait_ge(added, HEADS * c + d + 1)
                        dve.tensor_reduce(tops[0:r, bass.ds(d, 1)], scores[0:r, :], AX_X, ALU.max).then_inc(top, 1)
                        dve.wait_ge(top, HEADS * c + d + 2)
                    dve.wait_ge(turned, c + 1)
                    dve.tensor_copy(shift[:, c * P:(c + 1) * P], turn[:]).then_inc(kept, 1)
                    dve.wait_ge(kept, c + 1)


def load_products(sp, qp_d, kp_d, q_at, q_n, q_sb, k_at, k_n, k_sb, done):
    rows = PARTS * H
    for a in range(PARTS):
        sp.dma_start(k_sb[a * rows:(a + 1) * rows, 0:k_n], bass.AP(kp_d, k_at, [[TOK, rows], [1, k_n]])).then_inc(done, 16)
        for b in range(PARTS):
            at = (PARTS * a + b) * H
            sp.dma_start(q_sb[at:at + H, 0:q_n], bass.AP(qp_d, a * H * TOK + q_at, [[TOK, H], [1, q_n]])).then_inc(done, 16)


def split_shift(nc, shift, shift_d):
    with ExitStack() as ctx:
        s = Scope(nc, ctx, "sh")
        parts = [s.sb(f"part{k}", [P, NP], BF16) for k in range(PARTS)]
        rest = s.sb("rest", [P, NP])
        steps, stored = s.sem("steps"), s.sem("stored")
        block = ctx.enter_context(nc.Block())

        @block.vector
        def _(dve):
            chain = Chain(dve, steps)
            dve.tensor_scalar(parts[0][:], shift[:], -1.0, None, ALU.mult).then_inc(steps, 1)
            chain.done()
            dve.scalar_tensor_tensor(out=rest[:], in0=shift[:], scalar=-1.0, in1=parts[0][:], op0=ALU.mult,
                                     op1=ALU.subtract).then_inc(steps, 1)
            chain.done()
            dve.tensor_copy(parts[1][:], rest[:]).then_inc(steps, 1)
            chain.done()
            dve.tensor_tensor(parts[2][:], rest[:], parts[1][:], ALU.subtract).then_inc(steps, 1)

        @block.sync
        def _(sp):
            sp.wait_ge(steps, 4)
            for k in range(PARTS):
                sp.dma_start(bass.AP(shift_d, k * HEADS * NP, [[NP, HEADS], [1, NP]]), parts[k][:]).then_inc(stored, 16)
            sp.wait_ge(stored, 16 * PARTS)


class Steps:

    LATE = 2
    EARLY = 1

    def __init__(self, products):
        pairs = (C - products) // 2
        assert 2 * pairs + products == C
        self.doubles = next(k for k in range(DOUBLES, 0, -1) if GROUP * pairs % k == 0)
        spread = sorted([((m + 0.5) / pairs, 2) for m in range(pairs)] + [((m + 0.5) / products, 1) for m in range(products)])
        self.n = GROUP * C
        self.units = []
        for _ in range(GROUP):
            for _, size in spread:
                first = sum(map(len, self.units))
                self.units.append(list(range(first, first + size)))
        self.unit = {n: u for u, steps in enumerate(self.units) for n in steps}
        self.is_product = [len(self.units[self.unit[n]]) == 1 for n in range(self.n)]
        summing = iter(range(C - products))
        product = iter(range(C - products, C))
        self.chunk = [next(product) if self.is_product[n] else next(summing) for n in range(C)]
        self.chunk *= GROUP
        self.order = sorted(range(self.n), key=lambda n: (n // C, n + (self.LATE + 0.5) * self.is_product[n]))
        self.place = [self.order.index(n) for n in range(self.n)]
        self.exp_order = sorted(range(len(self.units)),
                                key=lambda u: self.units[u][-1] - (self.EARLY + 0.5) * (len(self.units[u]) == 1))
        self.exp_place = [self.exp_order.index(u) for u in range(len(self.units))]

    def buffer(self, n):
        return n % self.n % SCORES

    def slot(self, n):
        n %= self.n
        same = [u for u, steps in enumerate(self.units) if (len(steps) == 1) == self.is_product[n]]
        return self.is_product[n], same.index(self.unit[n]) % (SINGLES if self.is_product[n] else self.doubles), n - self.units[self.unit[n]][0]

    def last_like(self, what, n):
        return next(m for m in range(n - 1, n - 2 * self.n, -1) if what(m) == what(n))

    def all_before(self, i, n):
        return self.n * i + n

    def of_kind_before(self, i, n, product):
        per_body = sum(x == product for x in self.is_product)
        ahead, n = divmod(n, self.n)
        return per_body * i + per_body * ahead + sum(x == product for x in self.is_product[:n])

    def exped_by(self, i, n):
        beside, n = divmod(n, self.n)
        return len(self.units) * i + len(self.units) * beside + self.exp_place[self.unit[n]] + 1

    def used_by(self, i, n):
        behind, n = divmod(n, self.n)
        return self.n * i + self.n * behind + self.place[n] + 1


def attend(nc, at_d, et_d, qp_d, kp_d, v_d, shift_d, o_d, over, when, products):
    with ExitStack() as ctx:
        s = Scope(nc, ctx, f"at{when}")
        at = s.sb("at", [P, C, NB])
        plan = Steps(products)
        doubles = [s.sb(f"double{k}", [P, 2, NB]) for k in range(plan.doubles)]
        singles = [s.sb(f"single{k}", [P, 1, NB]) for k in range(SINGLES if products else 0)]
        q = [s.sb(f"q{k}", [P, NB], BF16) for k in range(2)]
        k_all = [s.sb(f"k{k}", [P, NP], BF16) for k in range(2)]
        v = [s.sb(f"v{k}", [P, C, VW]) for k in range(2)]
        o = [s.sb(f"o{k}", [P, QW]) for k in range(2)]
        score = [s.ps(f"score{k}", [P, -(-NB // BANK) * BANK]) for k in range(SCORES)]
        acc = [s.ps(f"acc{k}", [P, BANK]) for k in range(2)]
        cleared, k_zero = s.sem("cleared"), s.sem("k_zero")
        at_loaded = [s.sem(f"at_loaded{g}") for g in range(-(-C // CHUNKS_AT_ONCE) + 1)]
        head_loaded = [s.sem(f"head_loaded{k}") for k in range(2)]
        scored = s.sem("scored")
        added = s.sem("added")
        exped = s.sem("exped")
        multiplied = s.sem("multiplied")
        used = s.sem("used")
        kept = s.sem("kept")
        stored = [s.sem(f"stored{k}") for k in range(2)]
        block = ctx.enter_context(nc.Block())
        STEPS = plan.n
        UNITS = len(plan.units)
        AHEAD = STEPS
        BODIES = HEADS // GROUP
        LOADS = 16 * (PARTS + PARTS * PARTS + 1 + 3)
        STORES = 16 * COLT
        CLEARED = 8
        SCORE_LEAD = 8
        KEEP_LAG = 5
        assert GROUP * products % SINGLES == 0 and GROUP % 2 == 0

        groups = []
        for product in (False, True):
            steps = [n for n in range(C) if plan.is_product[n] == product]
            groups += [steps[m:m + CHUNKS_AT_ONCE] for m in range(0, len(steps), CHUNKS_AT_ONCE)]
        groups.sort(key=lambda steps: steps[-1])
        first_of_group = {steps[0]: g for g, steps in enumerate(groups)}

        def slot(n):
            product, buffer, half = plan.slot(n)
            return (singles if product else doubles)[buffer][:, half, :]

        def runs(eng):
            return eng.If(eng.value_load(over[0:1, 0:1], min_val=0, max_val=1) == when)

        @block.sync
        def _(sp):
            def load_adjacency(b, which):
                for g in which:
                    steps = groups[g]
                    product, first, count = plan.is_product[steps[0]], plan.chunk[steps[0]], len(steps)
                    if b:
                        sp.wait_ge(multiplied if product else added,
                                   plan.of_kind_before(b * BODIES - 1, STEPS - C + steps[-1] + 1, product))
                    src = (bass.AP(et_d, (first - C + products) * NP + b * NB, [[products * NP, P], [NP, count], [1, NB]]) if product
                           else bass.AP(at_d, first * NP + b * NB, [[C * NP, P], [NP, count], [1, NB]]))
                    sp.dma_start(at[:, first:first + count, :], src).then_inc(at_loaded[g], 16)

            def load(b, d, k):
                load_products(sp, qp_d, kp_d, d * N + b * NB, NB, q[k], d * N, N, k_all[k], head_loaded[k])
                sp.dma_start(q[k][SHIFT_ROW:SHIFT_ROW + PARTS, :],
                             bass.AP(shift_d, d * NP + b * NB, [[HEADS * NP, PARTS], [1, NB]])).then_inc(head_loaded[k], 16)
                sp.dma_start(v[k][:, 0:C - 1, :].rearrange("p j w -> p (j w)"),
                             bass.AP(v_d, d * (N * VW), [[C * VW, P], [1, (C - 1) * VW]])).then_inc(head_loaded[k], 16)
                for x, y in row_pieces(LAST):
                    sp.dma_start(v[k][x:y, C - 1, :], bass.AP(v_d, d * (N * VW) + (x * C + C - 1) * VW,
                                                              [[C * VW, y - x], [1, VW]])).then_inc(head_loaded[k], 16)

            def store(b, d, k):
                sp.wait_ge(kept, d + (b * HEADS + 1 + 2))
                for t in range(COLT):
                    width = min(QW, N - b * NB - t * QW)
                    sp.dma_start(bass.AP(o_d, d * N + (b * NB + t * QW), [[TOK, VW], [1, width]]),
                                 o[k][32 * t:32 * t + VW, 0:width]).then_inc(stored[k], 16)

            with runs(sp):
                for k in range(2):
                    sp.sem_inc(stored[k], STORES)
                load_adjacency(0, range(2))
                sp.wait_ge(cleared, CLEARED)
                for k in range(2):
                    load(0, k, k)
                load_adjacency(0, range(2, len(groups)))
                for b in range(BLOCKS):
                    with sp.Fori(0, HEADS // 2 - 1) as i:
                        for k in range(2):
                            sp.wait_ge(used, i * (2 * C) + ((b * HEADS + k + 1) * C + AHEAD))
                            load(b, 2 * i + (k + 2), k)
                            store(b, 2 * i + k, k)
                    for k in range(2):
                        if b + 1 < BLOCKS:
                            sp.wait_ge(used, ((b + 1) * HEADS - 1 + k) * C + AHEAD)
                            load(b + 1, k, k)
                            if k == 0:
                                load_adjacency(b + 1, range(len(groups)))
                        store(b, HEADS - 2 + k, k)
                for k in range(2):
                    sp.wait_ge(stored[k], STORES * (BLOCKS * HEADS // 2 + 1))

        @block.gpsimd
        def _(pool):
            with runs(pool):
                pool.memset(k_all[1][:], 0.0).then_inc(k_zero, 1)
                if not products:
                    return
                for b in range(BLOCKS):
                    with pool.Fori(0, BODIES) as i:
                        for n in range(STEPS):
                            if plan.is_product[n]:
                                if n in first_of_group:
                                    pool.wait_ge(at_loaded[first_of_group[n]], 16 * (b + 1))
                                pool.wait_ge(exped, plan.exped_by(i, n) + b * BODIES * UNITS)
                                pool.tensor_tensor(slot(n), slot(n), at[:, plan.chunk[n], :],
                                                   ALU.mult).then_inc(multiplied, 1)

        @block.tensor
        def _(pe):
            def scores(i, n):
                head, step = divmod(n % STEPS, C)
                k = head % 2
                if step == 0:
                    pe.wait_ge(head_loaded[k], LOADS * (GROUP // 2) * i + LOADS * (n // C // 2 + 1))
                if not (isinstance(i, int) and i == 0 and n < SCORES):
                    m = plan.last_like(plan.buffer, n)
                    if plan.is_product[m % STEPS]:
                        pe.wait_ge(exped, plan.exped_by(i, m))
                    else:
                        pe.wait_ge(added, plan.of_kind_before(i, m + 1, False))
                keys = k_all[k][:].rearrange("r (p j) -> r j p", j=C)[:, plan.chunk[n % STEPS], :]
                for a, b in col_pieces(NB):
                    last = pe.matmul(score[plan.buffer(n)][:, a:b], keys, q[k][:, a:b], start=True, stop=True)
                last.then_inc(scored, 1)

            def values(i, m):
                n = plan.order[m]
                head, step = divmod(n, C)
                k = head % 2
                if m % C == 0:
                    pe.wait_ge(kept, GROUP * i + (head + 1))
                if plan.is_product[n]:
                    pe.wait_ge(multiplied, plan.of_kind_before(i, n + 1, True))
                else:
                    pe.wait_ge(exped, plan.exped_by(i, n))
                for t in range(COLT):
                    last = pe.matmul(acc[k][32 * t:32 * t + VW, 0:QW], v[k][:, plan.chunk[n % STEPS], :],
                                     slot(n)[:, t * QW:(t + 1) * QW],
                                     start=(m % C == 0), stop=(m % C == C - 1), tile_position=(0, 32 * t))
                last.then_inc(used, 1)

            def body(i, more):
                for n in range(STEPS):
                    if n + SCORE_LEAD < STEPS or more:
                        scores(i, n + SCORE_LEAD)
                    values(i, n)

            with runs(pe):
                pe.sem_inc(used, AHEAD)
                pe.wait_ge(cleared, CLEARED)
                for n in range(SCORE_LEAD):
                    scores(0, n)
                with pe.Fori(0, BLOCKS * BODIES - 1) as i:
                    body(i, True)
                body(BLOCKS * BODIES - 1, False)

        @block.vector
        def _(dve):
            with runs(dve):
                dve.memset(k_all[0][:], 0.0).then_inc(k_zero, 1)
                for k in range(2):
                    dve.memset(q[k][:], 0.0).then_inc(cleared, 1)
                    dve.memset(v[k][:, C - 1, :], 0.0).then_inc(cleared, 1)
                    dve.memset(acc[k][:, 0:QW], 0.0).then_inc(cleared, 1)
                dve.wait_ge(k_zero, 2)
                for k in range(2):
                    dve.memset(k_all[k][SHIFT_ROW:SHIFT_ROW + PARTS, 0:N], 1.0).then_inc(cleared, 1)
                for b in range(BLOCKS):
                    with dve.Fori(0, BODIES) as i:
                        for n in range(STEPS):
                            if not plan.is_product[n]:
                                if n in first_of_group:
                                    dve.wait_ge(at_loaded[first_of_group[n]], 16 * (b + 1))
                                dve.wait_ge(scored, plan.all_before(i, n) + (b * BODIES * STEPS + 1))
                                dve.wait_ge(used, plan.used_by(i, plan.last_like(plan.slot, n)) + (b * BODIES * STEPS + AHEAD))
                                dve.scalar_tensor_tensor(out=slot(n), in0=at[:, plan.chunk[n], :], scalar=2.0,
                                                         in1=score[plan.buffer(n)][:, 0:NB], op0=ALU.mult, op1=ALU.add).then_inc(added, 1)

        @block.scalar
        def _(act):
            def exponential(i, m):
                ahead, m = divmod(m, UNITS)
                steps = [n + ahead * STEPS for n in plan.units[plan.exp_order[m]]]
                product, buffer, _ = plan.slot(steps[0])
                if product:
                    n = steps[0]
                    act.wait_ge(scored, plan.all_before(i, n + 1))
                    act.wait_ge(used, plan.used_by(i, plan.last_like(plan.slot, n)) + AHEAD)
                    act.activation(slot(n), score[plan.buffer(n)][:, 0:NB], ACT.Exp).then_inc(exped, 1)
                else:
                    act.wait_ge(added, plan.of_kind_before(i, steps[-1] + 1, False))
                    act.activation(doubles[buffer][:], doubles[buffer][:], ACT.Exp).then_inc(exped, 1)

            def keep_head(i, head):
                act.wait_ge(used, STEPS * i + ((head + 1) * C + AHEAD))
                act.wait_ge(stored[head % 2], STORES * (GROUP // 2) * i + STORES * (head // 2 + 1))
                act.activation(o[head % 2][:], acc[head % 2][:, 0:QW], ACT.Copy).then_inc(kept, 1)

            def body(i, more):
                for m in range(KEEP_LAG, UNITS + KEEP_LAG):
                    if m < UNITS or more:
                        exponential(i, m)
                    if m % (UNITS // GROUP) == KEEP_LAG - 1:
                        keep_head(i, m // (UNITS // GROUP) - 1)

            with runs(act):
                act.sem_inc(kept, 2)
                for m in range(KEEP_LAG):
                    exponential(0, m)
                with act.Fori(0, BLOCKS * BODIES - 1) as i:
                    body(i, True)
                body(BLOCKS * BODIES - 1, False)


def project_out(nc, o_d, out, keep):
    with ExitStack() as ctx:
        s = Scope(nc, ctx, "po")
        raw = [s.sb(f"raw{k}", [P, VW, P]) for k in range(2)]
        inv = s.sb("inv", [P, P])
        scaled = [s.sb(f"scaled{k}", [P, H, P]) for k in range(2)]
        turned = [s.sb(f"turned{k}", [P, H, P]) for k in range(2)]
        result = [s.sb(f"result{k}", [P, F]) for k in range(2)]
        tp = [s.ps(f"tp{k}", [P, H, P]) for k in range(2)]
        py = [s.ps(f"py{k}", [P, BANK]) for k in range(2)]
        loaded = [s.sem(f"loaded{k}") for k in range(2)]
        stored, result_free = s.sem("stored"), s.sem("result_free")
        cleared, inverted, divided, turned_ready, turned_kept, product, added = [
            s.sem(n) for n in ("cleared", "inverted", "divided", "turned_ready", "turned_kept", "product", "added")]
        block = ctx.enter_context(nc.Block())

        def rows_of(c):
            return LAST if isinstance(c, int) and c == C - 1 else P

        @block.sync
        def _(sp):
            def load(c, k):
                sp.wait_ge(divided, c + 1)
                for a, b in ([(0, P)] if rows_of(c) == P else row_pieces(LAST)):
                    sp.dma_start(raw[k][a:b, :, :], bass.AP(o_d, c * (P * P) + a * P, [[P, b - a], [TOK, VW], [1, P]])).then_inc(loaded[k], 16)

            sp.wait_ge(cleared, 2)
            with sp.Fori(0, C // 2 - 1) as i:
                for k in range(2):
                    load(2 * i + k, k)
            for c in (C - 2, C - 1):
                load(c, c % 2)

        @block.gpsimd
        def _(pool):
            def store(c, k):
                pool.wait_ge(added, c + 3)
                r = rows_of(c)
                pool.dma_start(bass.AP(out.tensor, c * (P * F), [[F, r], [1, F]]), result[k][0:r, :]).then_inc(stored, 16)
                pool.wait_ge(stored, 16 * c + 16)
                pool.sem_inc(result_free, 1)

            pool.sem_inc(result_free, 2)
            with pool.Fori(0, C // 2 - 1) as i:
                for k in range(2):
                    store(2 * i + k, k)
            for c in (C - 2, C - 1):
                store(c, c % 2)

        @block.tensor
        def _(pe):
            def turn(c, k):
                pe.wait_ge(divided, c + 3)
                pe.wait_ge(turned_kept, c + 1)
                for h in range(H):
                    last = pe.transpose(tp[k][:, h, :], scaled[k][:, h, :], keep["ident"][:])
                last.then_inc(turned_ready, 1)

            def project_back(c, k):
                pe.wait_ge(turned_kept, c + 3)
                pe.wait_ge(added, c + 1)
                for h in range(H):
                    last = pe.matmul(py[k][:, 0:F], turned[k][:, h, :], keep["wo_t"][:, h, :], start=(h == 0), stop=(h == H - 1))
                last.then_inc(product, 1)

            pe.sem_inc(turned_ready, 2)
            pe.sem_inc(product, 2)
            turn(0, 0)
            with pe.Fori(0, C // 2 - 1) as i:
                for k in range(2):
                    turn(2 * i + k + 1, 1 - k)
                    project_back(2 * i + k, k)
            turn(C - 1, 1)
            project_back(C - 2, 0)
            project_back(C - 1, 1)

        @block.scalar
        def _(act):
            act.sem_inc(turned_kept, 2)
            with act.Fori(0, C // 2) as i:
                for k in range(2):
                    c = 2 * i + k
                    act.wait_ge(turned_ready, c + 3)
                    act.wait_ge(product, c + 1)
                    act.activation(turned[k][:], tp[k][:], ACT.Copy).then_inc(turned_kept, 1)

        @block.vector
        def _(dve):
            dve.sem_inc(divided, 2)
            dve.sem_inc(added, 2)
            for k in range(2):
                dve.memset(raw[k][:], 1.0).then_inc(cleared, 1)

            def divide(c, k, count):
                dve.wait_ge(loaded[k], count)
                dve.wait_ge(divided, c + 2)
                dve.reciprocal(inv[:], raw[k][:, H, :]).then_inc(inverted, 1)
                dve.wait_ge(inverted, c + 1)
                dve.wait_ge(turned_ready, c + 1)
                dve.tensor_tensor(scaled[k][:], raw[k][:, 0:H, :], inv[:].unsqueeze(1).to_broadcast([P, H, P]),
                                  ALU.mult).then_inc(divided, 1)

            def add(c, k):
                dve.wait_ge(product, c + 3)
                dve.wait_ge(result_free, c + 1)
                dve.tensor_tensor(result[k][:], py[k][:, 0:F], keep["x"][:, c, :], ALU.add).then_inc(added, 1)

            for k in range(2):
                divide(k, k, 16)
            with dve.Fori(0, C // 2 - 2) as i:
                for k in range(2):
                    divide(2 * i + k + 2, k, 16 * i + 32)
                    add(2 * i + k, k)
            for c in range(C - 4, C):
                if c + 2 < C:
                    divide(c + 2, c % 2, 16 * ((c + 2) // 2 + 1) + (16 if c + 2 == C - 1 else 0))
                add(c, c % 2)


def gnn_two_layers(nc, x, adj, w_in, w_out, wq, wk, wv, wo, out):
    at_d = nc.dram_tensor("adj_t_scratch", (P, C, NP), F32)
    et_d = nc.dram_tensor("exp_adj_t_scratch", (P, PRODUCTS, NP), F32)
    amax_d = nc.dram_tensor("amax_scratch", (NP,), F32)
    qp_d = nc.dram_tensor("q_parts_scratch", (PARTS, H, TOK), BF16)
    kp_d = nc.dram_tensor("k_parts_scratch", (PARTS, H, TOK), BF16)
    v_d = nc.dram_tensor("v_scratch", (TOK, VW), F32)
    nq_d = nc.dram_tensor("q_norm_scratch", (TOK,), F32)
    nk_d = nc.dram_tensor("k_norm_scratch", (TOK,), F32)
    shift_d = nc.dram_tensor("shift_scratch", (PARTS, HEADS, NP), BF16)
    o_d = nc.dram_tensor("attended_scratch", (VW, TOK), F32)
    with ExitStack() as ctx:
        s = Scope(nc, ctx, "all")
        keep = {"x": s.sb("x", [P, C, F]), "ident": s.sb("ident", [P, P]), "ones": s.sb("ones", [P, 1]),
                "wo_t": s.sb("wo_t", [P, H, P])}
        over = s.sb("over", [1, 1], I32)
        with ExitStack() as early:
            e = Scope(nc, early, "early")
            keep |= {"h_nat": e.sb("h_nat", [P, C, F]), "w_t": e.sb("w_t", [P, 3 * H * P]), "h_t": e.sb("h_t", [P, NP])}
            with ExitStack() as layer:
                y = Scope(nc, layer, "layer1")
                keep |= {"h_int": y.sb("h_int", [P, C, F]), "in_acc": y.sb("in_acc", [P, NP]),
                         "out_acc": y.sb("out_acc", [P, NP]), "col_acc": y.sb("col_acc", [P, NP]),
                         "row_sum": y.sb("row_sum", [P, C])}
                load_and_norm_first(nc, x, keep)
                stream_adjacency(nc, adj, at_d, et_d, amax_d, keep)
                finish_first_layer(nc, w_in, w_out, wq, wk, wv, wo, keep)
            project(nc, qp_d, kp_d, v_d, nq_d, nk_d, keep)
        with ExitStack() as middle:
            m = Scope(nc, middle, "softmax")
            shift = m.sb("shift", [P, NP])
            bound_scores(nc, nq_d, nk_d, amax_d, shift, over)
            take_true_maxima(nc, adj, qp_d, kp_d, shift, over, keep["ident"])
            split_shift(nc, shift, shift_d)
        attend(nc, at_d, et_d, qp_d, kp_d, v_d, shift_d, o_d, over, 0, PRODUCTS)
        attend(nc, at_d, et_d, qp_d, kp_d, v_d, shift_d, o_d, over, 1, 0)
        project_out(nc, o_d, out, keep)


_INS = ["x", "adj", "L0_gnn_W_in", "L0_gnn_W_out", "L1_gnn_Wq", "L1_gnn_Wk", "L1_gnn_Wv", "L1_gnn_Wo"]
_OUTS = [((N, F), "float32")]


def kernel(**inputs):
    import numpy as _np
    import concourse.bacc as _bacc
    from concourse import mybir as _mybir
    from concourse.bass_utils import run_bass_kernel_spmd as _run

    nc = _bacc.Bacc("TRN2", target_bir_lowering=False, num_devices=1)
    arrays, args = {}, []
    for name in _INS:
        a = _np.ascontiguousarray(inputs[name])
        arrays[f"in_{name}_dram"] = a
        args.append(nc.dram_tensor(f"in_{name}_dram", a.shape, _mybir.dt.from_np(a.dtype), kind="ExternalInput").ap())
    for i, (shape, dtype) in enumerate(_OUTS):
        dt = _mybir.dt.from_np(_np.dtype(dtype))
        args.append(nc.dram_tensor(f"out_{i}_dram", shape, dt, kind="ExternalOutput").ap())
    gnn_two_layers(nc, *args)
    r = _run(nc, [arrays], core_ids=[0])
    got = tuple(r.results[0][f"out_{i}_dram"] for i in range(len(_OUTS)))
    return got[0]
```

```python
from contextlib import ExitStack

import concourse.bass as bass
from concourse import mybir

ALU = mybir.AluOpType
ACT = mybir.ActivationFunctionType
F32 = mybir.dt.float32
BF16 = mybir.dt.bfloat16
I32 = mybir.dt.int32
AX_X = mybir.AxisListType.X

P = 128
N = 3327
F = 128
H = 8
HEADS = 128
C = -(-N // P)
NP = C * P
LAST = N - (C - 1) * P
TOK = NP * P
BANK = 512
EPS = 1e-5
SCALE = float(F) ** -0.5

BLOCKS = 4
NB = -(-N // BLOCKS)
assert N <= NB * BLOCKS <= NP
SCORES = 3
PARTS = 3
SHIFT_ROW = 96
VW = H + 1
COLT = 4
QW = NB // COLT
assert QW * COLT == NB
DOUBLES = 8
SINGLES = 4
GROUP = 4
CHUNKS_AT_ONCE = 5
PRODUCTS = 6
LIMIT = 30.0


def row_pieces(total):
    whole = total // 16 * 16
    return [(0, whole)] + ([(whole, total)] if total > whole else [])


def col_pieces(width):
    return [(a, min(a + BANK, width)) for a in range(0, width, BANK)]


def normalise(dve, x, h, centred, stats, chain, rooted, variance_ready, root_count):
    step = chain
    dve.tensor_reduce(stats[:, 0, :], x, AX_X, ALU.add).then_inc(step.sem, 1)
    step.done()
    dve.tensor_scalar(stats[:, 0, :], stats[:, 0, :], 1.0 / F, None, ALU.mult).then_inc(step.sem, 1)
    step.done()
    for c in range(C):
        last = dve.tensor_scalar(centred[:, c, :], x[:, c, :], stats[:, 0, c:c + 1], None, ALU.subtract)
    last.then_inc(step.sem, 1)
    step.done()
    dve.tensor_tensor(h, centred[:], centred[:], ALU.mult).then_inc(step.sem, 1)
    step.done()
    dve.tensor_reduce(stats[:, 1, :], h, AX_X, ALU.add).then_inc(step.sem, 1)
    step.done()
    dve.tensor_scalar(stats[:, 1, :], stats[:, 1, :], 1.0 / F, EPS, ALU.mult, ALU.add).then_inc(variance_ready, 1)
    dve.wait_ge(rooted, root_count)
    dve.reciprocal(stats[:, 3, :], stats[:, 2, :]).then_inc(step.sem, 1)
    step.done()
    for c in range(C):
        last = dve.tensor_scalar(h[:, c, :], centred[:, c, :], stats[:, 3, c:c + 1], 0.0, ALU.mult, ALU.max)
    last.then_inc(step.sem, 1)
    step.done()


class Chain:

    def __init__(self, engine, sem):
        self.engine, self.sem, self.count = engine, sem, 0

    def done(self):
        self.count += 1
        self.engine.wait_ge(self.sem, self.count)


class Scope:

    def __init__(self, nc, ctx, tag):
        self.nc, self.ctx, self.tag = nc, ctx, tag

    def sb(self, name, shape, dt=F32):
        return self.ctx.enter_context(self.nc.sbuf_tensor(f"{self.tag}_{name}", shape, dt))

    def ps(self, name, shape, dt=F32):
        return self.ctx.enter_context(self.nc.psum_tensor(f"{self.tag}_{name}", shape, dt))

    def sem(self, name):
        return self.ctx.enter_context(self.nc.semaphore(f"{self.tag}_{name}"))


def load_and_norm_first(nc, x, keep):
    with ExitStack() as ctx:
        s = Scope(nc, ctx, "n1")
        x_int = s.sb("x_int", [P, C, F])
        centred = [s.sb(f"centred{k}", [P, C, F]) for k in range(2)]
        stats = s.sb("stats", [P, 4, 2, C])
        cleared, nat_loaded, int_loaded = s.sem("cleared"), s.sem("nat_loaded"), s.sem("int_loaded")
        int_mean, int_squared, variance_ready, rooted = [s.sem(n) for n in ("int_mean", "int_squared", "variance_ready", "rooted")]
        inverted, int_centred, steps = s.sem("inverted"), s.sem("int_centred"), s.sem("steps")
        ident_zero, ident_done = s.sem("ident_zero"), s.sem("ident_done")
        x_nat, h_nat, h_int = keep["x"], keep["h_nat"], keep["h_int"]
        block = ctx.enter_context(nc.Block())
        pieces = row_pieces(LAST)

        @block.sync
        def _(sp):
            sp.wait_ge(cleared, 2)
            sp.dma_start(x_nat[:, 0:C - 1, :], x[0:(C - 1) * P, :].rearrange("(c p) f -> p c f", p=P)).then_inc(nat_loaded, 16)
            for a, b in pieces:
                sp.dma_start(x_nat[a:b, C - 1, :], x[(C - 1) * P + a:(C - 1) * P + b, :]).then_inc(nat_loaded, 16)
            for a, b in pieces:
                sp.dma_start(x_int[a:b, :, :], x[C * a:C * b, :].rearrange("(p j) f -> p j f", j=C)).then_inc(int_loaded, 16)
            sp.dma_start(x_int[P - 1:P, 0:C - 1, :],
                         x[C * (P - 1):N, :].rearrange("(p j) f -> p j f", p=1)).then_inc(int_loaded, 16)

        @block.gpsimd
        def _(pool):
            pool.memset(keep["ident"][:], 0.0).then_inc(ident_zero, 1)
            pool.wait_ge(ident_zero, 1)
            pool.affine_select(out=keep["ident"][:], in_=keep["ident"][:], compare_op=ALU.not_equal, fill=1.0,
                               base=0, pattern=[[-1, P]], channel_multiplier=1).then_inc(ident_done, 1)

        @block.scalar
        def _(act):
            act.wait_ge(int_mean, 1)
            for c in range(C):
                last = act.activation(centred[1][:, c, :], x_int[:, c, :], ACT.Identity, bias=stats[:, 0, 1, c:c + 1])
            last.then_inc(int_centred, 1)
            act.wait_ge(int_centred, 1)
            act.activation(h_int[:], centred[1][:], ACT.Square).then_inc(int_squared, 1)
            act.wait_ge(variance_ready, 1)
            act.activation(stats[:, 2, :, :], stats[:, 1, :, :], ACT.Sqrt).then_inc(rooted, 1)
            act.wait_ge(inverted, 1)
            for c in range(C):
                act.activation(h_int[:, c, :], centred[1][:, c, :], ACT.Relu, scale=stats[:, 3, 1, c:c + 1])

        @block.vector
        def _(dve):
            dve.memset(keep["ones"][:], 1.0)
            dve.memset(x_nat[:, C - 1, :], 0.0).then_inc(cleared, 1)
            dve.memset(x_int[:, C - 1, :], 0.0).then_inc(cleared, 1)
            chain = Chain(dve, steps)
            dve.wait_ge(nat_loaded, 16 * (1 + len(pieces)))
            dve.tensor_reduce(stats[:, 0, 0, :], x_nat[:], AX_X, ALU.add)
            dve.wait_ge(int_loaded, 16 * (1 + len(pieces)))
            dve.tensor_reduce(stats[:, 0, 1, :], x_int[:], AX_X, ALU.add).then_inc(steps, 1)
            chain.done()
            dve.tensor_scalar(stats[:, 0, 1, :], stats[:, 0, 1, :], -1.0 / F, None, ALU.mult).then_inc(int_mean, 1)
            dve.tensor_scalar(stats[:, 0, 0, :], stats[:, 0, 0, :], 1.0 / F, None, ALU.mult).then_inc(steps, 1)
            chain.done()
            for c in range(C):
                last = dve.tensor_scalar(centred[0][:, c, :], x_nat[:, c, :], stats[:, 0, 0, c:c + 1], None, ALU.subtract)
            last.then_inc(steps, 1)
            chain.done()
            dve.tensor_tensor(h_nat[:], centred[0][:], centred[0][:], ALU.mult).then_inc(steps, 1)
            chain.done()
            dve.tensor_reduce(stats[:, 1, 0, :], h_nat[:], AX_X, ALU.add)
            dve.wait_ge(int_squared, 1)
            dve.tensor_reduce(stats[:, 1, 1, :], h_int[:], AX_X, ALU.add).then_inc(steps, 1)
            chain.done()
            dve.tensor_scalar(stats[:, 1, :, :], stats[:, 1, :, :], 1.0 / F, EPS, ALU.mult, ALU.add).then_inc(variance_ready, 1)
            dve.wait_ge(rooted, 1)
            dve.reciprocal(stats[:, 3, :, :], stats[:, 2, :, :]).then_inc(inverted, 1)
            dve.wait_ge(inverted, 1)
            for c in range(C):
                dve.tensor_scalar(h_nat[:, c, :], centred[0][:, c, :], stats[:, 3, 0, c:c + 1], 0.0, ALU.mult, ALU.max)


def stream_adjacency(nc, adj, at_d, et_d, amax_d, keep):
    with ExitStack() as ctx:
        s = Scope(nc, ctx, "st")
        a_rows = [s.sb(f"a_rows{k}", [P, NP]) for k in range(2)]
        a_t = [s.sb(f"a_t{k}", [P, C, P]) for k in range(2)]
        e_t = [s.sb(f"e_t{k}", [P, PRODUCTS, P]) for k in range(2)]
        h_now = [s.sb(f"h_now{k}", [P, F]) for k in range(2)]
        zero_row = s.sb("zero_row", [1, NP])
        row_max = s.sb("row_max", [P, C])
        tp = [s.ps(f"tp{k}", [P, BANK]) for k in range(2)]
        out_sum = [s.ps(f"out_sum{k}", [P, BANK]) for k in range(2)]
        in_sum = [s.ps(f"in_sum{k}", [P, BANK]) for k in range(2)]
        padding_zero, zero_row_set = s.sem("padding_zero"), s.sem("zero_row_set")
        a_loaded = [s.sem(f"a_loaded{k}") for k in range(2)]
        last_loaded, max_stored = s.sem("last_loaded"), s.sem("max_stored")
        h_copied, at_copied = s.sem("h_copied"), s.sem("at_copied")
        at_stored = [s.sem(f"at_stored{k}") for k in range(2)]
        transposed, out_ready, out_added = s.sem("transposed"), s.sem("out_ready"), s.sem("out_added")
        in_ready, in_copied = s.sem("in_ready"), s.sem("in_copied")
        dve_read, pool_added, out_zero = s.sem("dve_read"), s.sem("pool_added"), s.sem("out_zero")
        block = ctx.enter_context(nc.Block())
        groups = [range(g, min(g + 4, C)) for g in range(0, C, 4)]
        G = len(groups)
        pieces = col_pieces(NP)
        assert len(pieces) == G
        FREE = 2

        @block.sync
        def _(sp):
            def load(c, k):
                sp.dma_start(a_rows[k][:, 0:N], bass.AP(adj.tensor, c * (P * N), [[N, P], [1, N]])).then_inc(a_loaded[k], 16)

            def store(c, k):
                sp.wait_ge(at_copied, G * c + G + FREE)
                sp.dma_start(bass.AP(at_d, c * P, [[C * NP, P], [NP, C], [1, P]]), a_t[k][:]).then_inc(at_stored[k], 16)
                sp.dma_start(bass.AP(et_d, c * P, [[PRODUCTS * NP, P], [NP, PRODUCTS], [1, P]]), e_t[k][:]).then_inc(at_stored[k], 16)

            def all_read(c):
                sp.wait_ge(in_ready, c + 1 + FREE)
                sp.wait_ge(dve_read, c + 1 + FREE)
                sp.wait_ge(pool_added, c + 1 + FREE)

            for k in range(2):
                sp.sem_inc(at_stored[k], 32)
            load(0, 0)
            load(1, 1)
            with sp.Fori(0, C // 2 - 2) as i:
                for k in range(2):
                    store(2 * i + k, k)
                    all_read(2 * i + k)
                    load(2 * i + k + 2, k)
            store(C - 4, 0)
            all_read(C - 4)
            load(C - 2, 0)
            store(C - 3, 1)
            all_read(C - 3)
            (_, whole), (_, rest) = row_pieces(LAST)
            sp.wait_ge(zero_row_set, 1)
            sp.dma_start(a_rows[1][LAST:P, :], zero_row[:]).then_inc(last_loaded, 16)
            sp.dma_start(a_rows[1][whole:rest, 0:N], adj[(C - 1) * P + whole:N, :]).then_inc(last_loaded, 16)
            sp.wait_ge(last_loaded, 32)
            sp.dma_start(a_rows[1][0:whole, 0:N], adj[(C - 1) * P:(C - 1) * P + whole, :]).then_inc(a_loaded[1], 16)
            store(C - 2, 0)
            store(C - 1, 1)
            sp.wait_ge(dve_read, C + FREE)
            sp.dma_start(bass.AP(amax_d, 0, [[1, P], [P, C], [1, 1]]), row_max[:].rearrange("p (c o) -> p c o", o=1),
                         allow_slow_non_contiguous=True).then_inc(max_stored, 16)
            sp.wait_ge(max_stored, 16)
            for k in range(2):
                sp.wait_ge(at_stored[k], 32 * (C // 2) + 32)

        @block.gpsimd
        def _(pool):
            pool.memset(keep["col_acc"][:], 0.0).then_inc(pool_added, FREE)
            pool.wait_ge(padding_zero, 2)
            with pool.Fori(0, C // 2) as i:
                for k in range(2):
                    c = 2 * i + k
                    pool.wait_ge(in_ready, c + 1)
                    pool.tensor_copy(h_now[k][:], keep["h_nat"][:, c, :]).then_inc(h_copied, 1)
                    pool.wait_ge(a_loaded[k], 16 * i + 16)
                    pool.wait_ge(pool_added, c + FREE)
                    pool.tensor_tensor(keep["col_acc"][:], keep["col_acc"][:], a_rows[k][:], ALU.add).then_inc(pool_added, 1)

        @block.tensor
        def _(pe):
            pe.sem_inc(in_ready, FREE)
            pe.wait_ge(padding_zero, 2)
            with pe.Fori(0, C // 2) as i:
                for k in range(2):
                    c = 2 * i + k
                    a_cols = a_rows[k][:].rearrange("p (q j) -> p j q", j=C)
                    pe.wait_ge(a_loaded[k], 16 * i + 16)
                    pe.wait_ge(h_copied, c + 1)
                    for g in range(G + 1):
                        if g < G:
                            pe.wait_ge(at_copied, G * c + g + 1)
                            for m, j in enumerate(groups[g]):
                                last = pe.transpose(tp[(G * k + g) % 2][:, m * P:(m + 1) * P], a_cols[:, j, :], keep["ident"][:])
                            last.then_inc(transposed, 1)
                            a, b = pieces[g]
                            pe.wait_ge(out_added, G * c + g + 1)
                            pe.matmul(out_sum[(G * k + g) % 2][:, 0:b - a], h_now[k][:], a_rows[k][:, a:b],
                                      start=True, stop=True).then_inc(out_ready, 1)
                        if g == 0:
                            continue
                        if g == 1:
                            pe.wait_ge(in_copied, c + 1)
                        pe.wait_ge(at_copied, G * c + g + FREE)
                        for j in groups[g - 1]:
                            last = pe.matmul(in_sum[k][:, 0:P], keep["h_int"][:, j, :], a_t[k][:, j, :],
                                             start=(j == 0), stop=(j == C - 1))
                    last.then_inc(in_ready, 1)

        @block.scalar
        def _(act):
            act.sem_inc(at_copied, FREE)
            act.sem_inc(in_copied, FREE)
            with act.Fori(0, C // 2) as i:
                for k in range(2):
                    c = 2 * i + k
                    act.wait_ge(in_ready, c + 1)
                    act.wait_ge(at_stored[k], 32 * i + 32)
                    for g in range(G):
                        j0, n = groups[g][0], len(groups[g])
                        act.wait_ge(transposed, G * c + g + 1)
                        e0 = max(j0, C - PRODUCTS)
                        if e0 < j0 + n:
                            act.activation(e_t[k][:, e0 - (C - PRODUCTS):j0 + n - (C - PRODUCTS), :].rearrange("p j n -> p (j n)"),
                                           tp[(G * k + g) % 2][:, (e0 - j0) * P:n * P], ACT.Exp, scale=2.0)
                        act.activation(a_t[k][:, j0:j0 + n, :].rearrange("p j n -> p (j n)"), tp[(G * k + g) % 2][:, 0:n * P],
                                       ACT.Copy).then_inc(at_copied, 1)
                    act.wait_ge(in_ready, c + 1 + FREE)
                    act.activation(keep["in_acc"][:, bass.ds(c * P, P)], in_sum[k][:, 0:P], ACT.Copy).then_inc(in_copied, 1)

        @block.vector
        def _(dve):
            dve.sem_inc(out_added, FREE)
            dve.sem_inc(dve_read, FREE)
            for k in range(2):
                dve.memset(a_rows[k][:, N:NP], 0.0).then_inc(padding_zero, 1)
            dve.memset(keep["out_acc"][:], 0.0).then_inc(out_zero, 1)
            dve.memset(zero_row[:], 0.0).then_inc(zero_row_set, 1)
            dve.wait_ge(padding_zero, 2)
            dve.wait_ge(out_zero, 1)
            with dve.Fori(0, C // 2) as i:
                for k in range(2):
                    c = 2 * i + k
                    dve.wait_ge(a_loaded[k], 16 * i + 16)
                    for g in range(G):
                        a, b = pieces[g]
                        dve.wait_ge(out_ready, G * c + g + 1)
                        dve.wait_ge(out_added, G * c + g + 1)
                        dve.tensor_tensor(keep["out_acc"][:, a:b], keep["out_acc"][:, a:b],
                                          out_sum[(G * k + g) % 2][:, 0:b - a], ALU.add).then_inc(out_added, 1)
                        if g == 1:
                            dve.tensor_reduce(keep["row_sum"][:, bass.ds(c, 1)], a_rows[k][:], AX_X, ALU.add)
                        if g == 4:
                            dve.tensor_reduce(row_max[:, bass.ds(c, 1)], a_rows[k][:], AX_X, ALU.max,
                                              apply_absolute_value=True).then_inc(dve_read, 1)


def finish_first_layer(nc, w_in, w_out, wq, wk, wv, wo, keep):
    with ExitStack() as ctx:
        s = Scope(nc, ctx, "fl")
        mix = s.sb("mix", [P, 2, F])
        w_nat = s.sb("w_nat", [P, 3, H, F])
        wo_nat = s.sb("wo_nat", [P, H * P])
        centred = s.sb("centred", [P, C, F])
        stats = s.sb("stats", [P, 4, C])
        degree = s.sb("degree", [P, 4, 2, C])
        y = s.ps("y", [P, 8 * BANK])
        deg = y[:, 7 * BANK:7 * BANK + C]
        mix_loaded, loaded, deg_ready = s.sem("mix_loaded"), s.sem("loaded"), s.sem("deg_ready")
        mixed, x_ready, steps = s.sem("mixed"), s.sem("x_ready"), s.sem("steps")
        variance_ready, rooted = s.sem("variance_ready"), s.sem("rooted")
        h_ready, h_turned, w_turned, w_kept = s.sem("h_ready"), s.sem("h_turned"), s.sem("w_turned"), s.sem("w_kept")
        banks = [range(c, min(c + BANK // P, C)) for c in range(0, C, BANK // P)]
        block = ctx.enter_context(nc.Block())
        x1, ident = keep["x"], keep["ident"]

        @block.sync
        def _(sp):
            sp.dma_start(mix[:, 0, :], w_in).then_inc(mix_loaded, 16)
            sp.dma_start(mix[:, 1, :], w_out).then_inc(mix_loaded, 16)
            for k, w in enumerate((wq, wk, wv)):
                sp.dma_start(w_nat[:, k, :, :], w.rearrange("(t h) f -> t h f", h=H)).then_inc(loaded, 16)
            sp.dma_start(wo_nat[:], wo).then_inc(loaded, 16)

        @block.tensor
        def _(pe):
            for c in range(C):
                last = pe.matmul(deg[:, c:c + 1], keep["col_acc"][:, c * P:(c + 1) * P], keep["ones"][:, 0:1],
                                 start=True, stop=True)
            last.then_inc(deg_ready, 1)
            pe.wait_ge(mix_loaded, 32)
            for k, acc in enumerate((keep["in_acc"], keep["out_acc"])):
                for n, bank in enumerate(banks):
                    if k:
                        pe.wait_ge(x_ready, n + 1)
                    for c in bank:
                        last = pe.matmul(y[:, c * P:(c + 1) * P], acc[:, c * P:(c + 1) * P], mix[:, k, :], start=True, stop=True)
                    last.then_inc(mixed, 1)
            pe.wait_ge(loaded, 16 * 4)
            pe.wait_ge(x_ready, 2 * len(banks))
            for k in range(3):
                for h in range(H):
                    at = (k * H + h) * P
                    last = pe.transpose(y[:, at:at + P], w_nat[:, k, h, :], ident[:])
            wo_cols = wo_nat[:].rearrange("o (t h) -> o h t", h=H)
            for h in range(H):
                at = (3 * H + h) * P
                last = pe.transpose(y[:, at:at + P], wo_cols[:, h, :], ident[:])
            last.then_inc(w_turned, 1)
            pe.wait_ge(w_kept, 1)
            pe.wait_ge(h_ready, 1)
            for c in range(C):
                last = pe.transpose(y[:, c * P:(c + 1) * P], keep["h_nat"][:, c, :], ident[:])
            last.then_inc(h_turned, 1)

        @block.scalar
        def _(act):
            act.wait_ge(w_turned, 1)
            act.activation(keep["w_t"][:], y[:, 0:6 * BANK], ACT.Copy)
            act.activation(keep["wo_t"][:].rearrange("p h o -> p (h o)"), y[:, 6 * BANK:8 * BANK], ACT.Copy).then_inc(w_kept, 1)
            act.wait_ge(variance_ready, 1)
            act.activation(stats[:, 2, :], stats[:, 1, :], ACT.Sqrt).then_inc(rooted, 1)
            act.wait_ge(h_turned, 1)
            act.activation(keep["h_t"][:, 4 * BANK:NP], y[:, 4 * BANK:NP], ACT.Copy)

        @block.vector
        def _(dve):
            chain = Chain(dve, steps)
            dve.tensor_copy(degree[:, 0, 0, :], keep["row_sum"][:])
            dve.wait_ge(deg_ready, 1)
            dve.tensor_copy(degree[:, 0, 1, :], deg).then_inc(steps, 1)
            chain.done()
            dve.tensor_scalar(degree[:, 1, :, :], degree[:, 0, :, :], 0.0, None, ALU.is_gt).then_inc(steps, 1)
            chain.done()
            dve.tensor_tensor(degree[:, 2, :, :], degree[:, 0, :, :], degree[:, 1, :, :], ALU.mult)
            dve.tensor_scalar(degree[:, 3, :, :], degree[:, 1, :, :], -1.0, 1.0, ALU.mult, ALU.add).then_inc(steps, 1)
            chain.done()
            dve.tensor_tensor(degree[:, 0, :, :], degree[:, 2, :, :], degree[:, 3, :, :], ALU.add).then_inc(steps, 1)
            chain.done()
            dve.reciprocal(degree[:, 1, :, :], degree[:, 0, :, :]).then_inc(steps, 1)
            chain.done()
            for k in range(2):
                for n, bank in enumerate(banks):
                    dve.wait_ge(mixed, k * len(banks) + n + 1)
                    if k:
                        dve.wait_ge(x_ready, n + 1)
                    for c in bank:
                        last = dve.scalar_tensor_tensor(out=x1[:, c, :], in0=y[:, c * P:(c + 1) * P], scalar=degree[:, 1, k, c:c + 1],
                                                        in1=x1[:, c, :], op0=ALU.mult, op1=ALU.add)
                    last.then_inc(x_ready, 1)
            dve.wait_ge(x_ready, 2 * len(banks))
            normalise(dve, x1[:], keep["h_nat"][:], centred, stats, chain, rooted, variance_ready, 1)
            dve.sem_inc(h_ready, 1)
            dve.wait_ge(h_turned, 1)
            dve.tensor_copy(keep["h_t"][:, 0:4 * BANK], y[:, 0:4 * BANK])


def project(nc, qp_d, kp_d, v_d, nq_d, nk_d, keep):
    with ExitStack() as ctx:
        s = Scope(nc, ctx, "pr")
        W = H * P
        parts = [[s.sb(f"parts{kind}{b}", [P, PARTS, H, 2, P], BF16) for kind in "qk"] for b in range(2)]
        rest = [s.sb(f"rest{kind}", [P, W]) for kind in "qk"]
        squares = [s.sb(f"squares{kind}", [P, W]) for kind in "qk"]
        value = [s.sb(f"value{k}", [P, P, VW]) for k in range(2)]
        norm2 = [s.sb(f"norm2{kind}", [P, C, P]) for kind in "qk"]
        h_now = [s.sb(f"h_now{k}", [P, P]) for k in range(2)]
        py = [s.ps(f"py{kind}", [P, W]) for kind in "qkv"]
        h_copied, product = s.sem("h_copied"), [s.sem(f"product_{kind}") for kind in "qkv"]
        rest_left, part2, part3 = [[s.sem(f"{n}_{kind}") for kind in "qk"] for n in ("rest_left", "part2", "part3")]
        squared, summed = [[s.sem(f"{n}_{kind}") for kind in "qk"] for n in ("squared", "summed")]
        value_kept, ones_set, rooted, norm_stored = s.sem("value_kept"), s.sem("ones_set"), s.sem("rooted"), s.sem("norm_stored")
        parts_stored = [[s.sem(f"parts_stored{b}{kind}") for kind in "qk"] for b in range(2)]
        value_stored = [s.sem(f"value_stored{k}") for k in range(2)]
        block = ctx.enter_context(nc.Block())
        PS = 16 * PARTS
        assert C % 4 == 2

        def over_chunks(eng, do):
            with eng.Fori(0, C // 4) as i:
                for k in range(4):
                    do(i, k)
            for k in range(2):
                do(C // 4, k)

        def by_head(tile):
            return tile[:].rearrange("p (h t) -> p h t", h=H)


        @block.sync
        def _(sp):
            for k in range(2):
                for kind in range(2):
                    sp.sem_inc(parts_stored[k][kind], PS)
                sp.sem_inc(value_stored[k], 16)

            def store(i, k):
                c, b = 4 * i + k, k // 2
                if k % 2 == 1:
                    for kind, dst in enumerate((qp_d, kp_d)):
                        sp.wait_ge(part3[kind], c + 2)
                        for part in range(PARTS):
                            sp.dma_start(bass.AP(dst, part * H * TOK + (c - 1) * P, [[C * P, P], [TOK, H], [1, 2 * P]]),
                                         parts[b][kind][:, part].rearrange("p h c t -> p h (c t)")).then_inc(parts_stored[b][kind], 16)
                sp.wait_ge(value_kept, c + 2)
                sp.dma_start(bass.AP(v_d, c * (P * VW), [[C * P * VW, P], [1, P * VW]]),
                             value[k % 2][:].rearrange("p t v -> p (t v)")).then_inc(value_stored[k % 2], 16)

            over_chunks(sp, store)
            sp.wait_ge(rooted, 2)
            for kind, dst in enumerate((nq_d, nk_d)):
                sp.dma_start(bass.AP(dst, 0, [[C * P, P], [1, C * P]]), norm2[kind][:].rearrange("p c t -> p (c t)")).then_inc(norm_stored, 16)
            sp.wait_ge(norm_stored, 32)
            for b in range(2):
                pairs = (C // 2 + 1 - b) // 2
                for kind in range(2):
                    sp.wait_ge(parts_stored[b][kind], PS * pairs + PS)
                sp.wait_ge(value_stored[b], 16 * (C // 2) + 16)

        @block.gpsimd
        def _(pool):
            for kind in range(2):
                pool.sem_inc(part3[kind], 1)
            h_cols = keep["h_t"][:].rearrange("f (p j) -> f j p", j=C)

            def copy_h(c, k):
                pool.wait_ge(product[2], c + 1)
                pool.tensor_copy(h_now[k][:], h_cols[:, bass.ds(c, 1), :].rearrange("f o p -> f (o p)")).then_inc(h_copied, 1)

            def third_parts(i, k):
                c, b, half = 4 * i + k, k // 2, k % 2
                if not (isinstance(i, int) and c == C - 1):
                    copy_h(c + 1, 1 - half)
                for kind in range(2):
                    pool.wait_ge(part2[kind], c + 1)
                    pool.tensor_tensor(parts[b][kind][:, 2, :, half, :], by_head(rest[kind]), parts[b][kind][:, 1, :, half, :],
                                       ALU.subtract).then_inc(part3[kind], 1)

            copy_h(0, 0)
            over_chunks(pool, third_parts)

        @block.tensor
        def _(pe):
            def products(i, k):
                c = 4 * i + k
                pe.wait_ge(h_copied, c + 1)
                for kind in range(3):
                    if kind < 2:
                        pe.wait_ge(rest_left[kind], c + 1)
                        pe.wait_ge(squared[kind], c + 1)
                    else:
                        pe.wait_ge(value_kept, c + 1)
                    for b in range(0, W, BANK):
                        last = pe.matmul(py[kind][:, b:b + BANK], h_now[k % 2][:], keep["w_t"][:, kind * W + b:kind * W + b + BANK],
                                         start=True, stop=True)
                    last.then_inc(product[kind], 1)

            pe.sem_inc(product[2], 2)
            over_chunks(pe, products)

        @block.scalar
        def _(act):
            def copies(i, k):
                c, b, half = 4 * i + k, k // 2, k % 2
                for kind in range(2):
                    if half == 0:
                        act.wait_ge(parts_stored[b][kind], PS * i + PS)
                    act.wait_ge(product[kind], c + 1)
                    act.activation(parts[b][kind][:, 0, :, half, :], by_head(py[kind]), ACT.Copy, scale=(SCALE, 1.0)[kind])
                    act.wait_ge(summed[kind], c + 1)
                    act.activation(squares[kind][:], py[kind][:], ACT.Square).then_inc(squared[kind], 1)
                for kind in range(2):
                    act.wait_ge(rest_left[kind], c + 2)
                    act.activation(parts[b][kind][:, 1, :, half, :], by_head(rest[kind]), ACT.Copy).then_inc(part2[kind], 1)

            for kind in range(2):
                act.sem_inc(squared[kind], 1)
            over_chunks(act, copies)
            for kind in range(2):
                act.wait_ge(summed[kind], C + 1)
                act.activation(norm2[kind][:], norm2[kind][:], ACT.Sqrt, scale=(SCALE * SCALE, 1.0)[kind]).then_inc(rooted, 1)

        @block.vector
        def _(dve):
            def rests(i, k):
                c, b, half = 4 * i + k, k // 2, k % 2
                for kind in range(2):
                    dve.wait_ge(squared[kind], c + 2)
                    dve.wait_ge(part3[kind], c + 1)
                    dve.scalar_tensor_tensor(out=by_head(rest[kind]), in0=by_head(py[kind]), scalar=(SCALE, 1.0)[kind],
                                             in1=parts[b][kind][:, 0, :, half, :], op0=ALU.mult,
                                             op1=ALU.subtract).then_inc(rest_left[kind], 1)
                    dve.tensor_reduce(norm2[kind][:, bass.ds(c, 1), :].rearrange("p o t -> p (o t)"),
                                      squares[kind][:].rearrange("p (h t) -> p t h", h=H),
                                      AX_X, ALU.add).then_inc(summed[kind], 1)
                dve.wait_ge(product[2], c + 3)
                dve.wait_ge(value_stored[k % 2], 32 * i + (16 * b + 16))
                dve.tensor_copy(value[k % 2][:, :, 0:H].rearrange("p t h -> p h t"), by_head(py[2])).then_inc(value_kept, 1)

            dve.sem_inc(value_kept, 1)
            for k in range(2):
                dve.memset(value[k][:], 1.0).then_inc(ones_set, 1)
            dve.wait_ge(ones_set, 2)
            for kind in range(2):
                dve.sem_inc(rest_left[kind], 1)
                dve.sem_inc(summed[kind], 1)
            over_chunks(dve, rests)


def load_group(sp, at_d, et_d, at, plan, g, b, done):
    steps = plan.groups[g]
    first, count, products = plan.chunk[steps[0]], len(steps), sum(plan.is_product[:C])
    if plan.is_product[steps[0]]:
        src = bass.AP(et_d, (first - C + products) * NP + b * NB, [[products * NP, P], [NP, count], [1, NB]])
    else:
        src = bass.AP(at_d, first * NP + b * NB, [[C * NP, P], [NP, count], [1, NB]])
    sp.dma_start(at[:, first:first + count, :], src).then_inc(done, 16)


def bound_scores(nc, nq_d, nk_d, amax_d, shift, over, ident, at, at_d, et_d, prefetched):
    with ExitStack() as ctx:
        s = Scope(nc, ctx, "bo")
        nq, nk, amax = s.sb("nq", [P, N]), s.sb("nk", [P, N]), s.sb("amax", [P, N])
        small, top = s.sb("small", [P, 2]), s.sb("top", [1, 2])
        turned = s.ps("turned", [P, P])
        nk_loaded, amax_loaded, nq_loaded, steps = [s.sem(n) for n in ("nk_loaded", "amax_loaded", "nq_loaded", "steps")]
        top_ready, top_turned = s.sem("top_ready"), s.sem("top_turned")
        block = ctx.enter_context(nc.Block())

        @block.sync
        def _(sp):
            for dst, src, step, done in ((nk, nk_d, N, nk_loaded), (amax, amax_d, 0, amax_loaded), (nq, nq_d, N, nq_loaded)):
                sp.dma_start(dst[:], bass.AP(src, 0, [[step, HEADS], [1, N]])).then_inc(done, 16)
            plan = Steps(PRODUCTS)
            for g in plan.prefetched:
                load_group(sp, at_d, et_d, at, plan, g, 0, prefetched)

        @block.tensor
        def _(pe):
            pe.wait_ge(top_ready, 1)
            pe.transpose(turned[0:1, :], small[:, 1:2], ident[:]).then_inc(top_turned, 1)

        @block.vector
        def _(dve):
            chain = Chain(dve, steps)
            dve.memset(shift[:, N:NP], 0.0)
            dve.wait_ge(nk_loaded, 16)
            dve.tensor_reduce(small[:, 0:1], nk[:], AX_X, ALU.max)
            dve.wait_ge(amax_loaded, 16)
            dve.tensor_scalar(amax[:], amax[:], 2.0, None, ALU.mult).then_inc(steps, 1)
            dve.wait_ge(nq_loaded, 16)
            chain.done()
            dve.scalar_tensor_tensor(out=shift[:, 0:N], in0=nq[:], scalar=small[:, 0:1], in1=amax[:], op0=ALU.mult,
                                     op1=ALU.add).then_inc(steps, 1)
            chain.done()
            dve.tensor_reduce(small[:, 1:2], shift[:, 0:N], AX_X, ALU.max).then_inc(top_ready, 1)
            dve.wait_ge(top_turned, 1)
            dve.tensor_reduce(top[:, 0:1], turned[0:1, :], AX_X, ALU.max).then_inc(steps, 1)
            chain.done()
            dve.tensor_scalar(top[:, 1:2], top[:, 0:1], LIMIT, None, ALU.is_gt).then_inc(steps, 1)
            chain.done()
            dve.tensor_copy(over[:], top[:, 1:2])


def take_true_maxima(nc, adj, qp_d, kp_d, shift, over, ident):
    with ExitStack() as ctx:
        s = Scope(nc, ctx, "mx")
        a_rows = s.sb("a_rows", [P, N])
        q = s.sb("q", [P, P], BF16)
        k_all = s.sb("k_all", [P, N], BF16)
        scores = s.sb("scores", [P, N])
        tops = s.sb("tops", [P, HEADS])
        py = s.ps("py", [P, 7 * BANK])
        turn = s.ps("turn", [P, P])
        a_loaded, qk_loaded, product, added, top = [s.sem(n) for n in ("a_loaded", "qk_loaded", "product", "added", "top")]
        turned, kept, zeroed, q_zero = s.sem("turned"), s.sem("kept"), s.sem("zeroed"), s.sem("q_zero")
        block = ctx.enter_context(nc.Block())
        LOADS = 16 * (3 + 9)

        def rows_of(c):
            return P if c < C - 1 else LAST

        @block.sync
        def _(sp):
            flag = sp.value_load(over[0:1, 0:1], min_val=0, max_val=1)
            with sp.If(flag != 0):
                sp.wait_ge(zeroed, 2)
                for c in range(C):
                    if c:
                        sp.wait_ge(kept, c)
                    for a, b in row_pieces(rows_of(c)):
                        sp.dma_start(a_rows[a:b, :], adj[c * P + a:c * P + b, :]).then_inc(a_loaded, 16)
                    with sp.Fori(0, HEADS) as d:
                        sp.wait_ge(top, HEADS * c + d + 1)
                        load_products(sp, qp_d, kp_d, d * N + c * P, rows_of(c), q, d * N, N, k_all, qk_loaded)

        @block.tensor
        def _(pe):
            flag = pe.value_load(over[0:1, 0:1], min_val=0, max_val=1)
            with pe.If(flag != 0):
                for c in range(C):
                    with pe.Fori(0, HEADS) as d:
                        pe.wait_ge(qk_loaded, LOADS * HEADS * c + LOADS * d + LOADS)
                        for a, b in col_pieces(N):
                            last = pe.matmul(py[:, a:b], q[:], k_all[:, a:b], start=True, stop=True)
                        last.then_inc(product, 1)
                    pe.wait_ge(top, HEADS * (c + 1) + 1)
                    pe.transpose(turn[:], tops[:], ident[:]).then_inc(turned, 1)

        @block.vector
        def _(dve):
            flag = dve.value_load(over[0:1, 0:1], min_val=0, max_val=1)
            with dve.If(flag != 0):
                dve.memset(q[:], 0.0).then_inc(zeroed, 1)
                dve.memset(k_all[:], 0.0).then_inc(zeroed, 1)
                dve.memset(tops[:], 0.0).then_inc(q_zero, 1)
                dve.wait_ge(q_zero, 1)
                dve.sem_inc(top, 1)
                for c in range(C):
                    r = rows_of(c)
                    dve.wait_ge(a_loaded, 16 * (c + 1) + (16 if c == C - 1 else 0))
                    with dve.Fori(0, HEADS) as d:
                        dve.wait_ge(product, HEADS * c + d + 1)
                        dve.scalar_tensor_tensor(out=scores[0:r, :], in0=a_rows[0:r, :], scalar=2.0, in1=py[0:r, 0:N],
                                                 op0=ALU.mult, op1=ALU.add).then_inc(added, 1)
                        dve.wait_ge(added, HEADS * c + d + 1)
                        dve.tensor_reduce(tops[0:r, bass.ds(d, 1)], scores[0:r, :], AX_X, ALU.max).then_inc(top, 1)
                        dve.wait_ge(top, HEADS * c + d + 2)
                    dve.wait_ge(turned, c + 1)
                    dve.tensor_copy(shift[:, c * P:(c + 1) * P], turn[:]).then_inc(kept, 1)
                    dve.wait_ge(kept, c + 1)


def load_products(sp, qp_d, kp_d, q_at, q_n, q_sb, k_at, k_n, k_sb, done):
    rows = PARTS * H
    for a in range(PARTS):
        sp.dma_start(k_sb[a * rows:(a + 1) * rows, 0:k_n], bass.AP(kp_d, k_at, [[TOK, rows], [1, k_n]])).then_inc(done, 16)
        for b in range(PARTS):
            at = (PARTS * a + b) * H
            sp.dma_start(q_sb[at:at + H, 0:q_n], bass.AP(qp_d, a * H * TOK + q_at, [[TOK, H], [1, q_n]])).then_inc(done, 16)


def split_shift(nc, shift, shift_d):
    with ExitStack() as ctx:
        s = Scope(nc, ctx, "sh")
        parts = [s.sb(f"part{k}", [P, NP], BF16) for k in range(PARTS)]
        rest = s.sb("rest", [P, NP])
        steps, stored = s.sem("steps"), s.sem("stored")
        block = ctx.enter_context(nc.Block())

        @block.vector
        def _(dve):
            chain = Chain(dve, steps)
            dve.tensor_scalar(parts[0][:], shift[:], -1.0, None, ALU.mult).then_inc(steps, 1)
            chain.done()
            dve.scalar_tensor_tensor(out=rest[:], in0=shift[:], scalar=-1.0, in1=parts[0][:], op0=ALU.mult,
                                     op1=ALU.subtract).then_inc(steps, 1)
            chain.done()
            dve.tensor_copy(parts[1][:], rest[:]).then_inc(steps, 1)
            chain.done()
            dve.tensor_tensor(parts[2][:], rest[:], parts[1][:], ALU.subtract).then_inc(steps, 1)

        @block.sync
        def _(sp):
            sp.wait_ge(steps, 4)
            for k in range(PARTS):
                sp.dma_start(bass.AP(shift_d, k * HEADS * NP, [[NP, HEADS], [1, NP]]), parts[k][:]).then_inc(stored, 16)
            sp.wait_ge(stored, 16 * PARTS)


class Steps:

    LATE = 2
    EARLY = 1

    def __init__(self, products):
        pairs = (C - products) // 2
        assert 2 * pairs + products == C
        self.doubles = next(k for k in range(DOUBLES, 0, -1) if GROUP * pairs % k == 0)
        spread = sorted([((m + 0.5) / pairs, 2) for m in range(pairs)] + [((m + 0.5) / products, 1) for m in range(products)])
        self.n = GROUP * C
        self.units = []
        for _ in range(GROUP):
            for _, size in spread:
                first = sum(map(len, self.units))
                self.units.append(list(range(first, first + size)))
        self.unit = {n: u for u, steps in enumerate(self.units) for n in steps}
        self.is_product = [len(self.units[self.unit[n]]) == 1 for n in range(self.n)]
        summing = iter(range(C - products))
        product = iter(range(C - products, C))
        self.chunk = [next(product) if self.is_product[n] else next(summing) for n in range(C)]
        self.chunk *= GROUP
        self.groups = []
        for kind in (False, True):
            steps = [n for n in range(C) if self.is_product[n] == kind]
            self.groups += [steps[m:m + CHUNKS_AT_ONCE] for m in range(0, len(steps), CHUNKS_AT_ONCE)]
        self.groups.sort(key=lambda steps: steps[-1])
        self.prefetched = [g for g, steps in enumerate(self.groups) if steps[0] < C // 3]
        self.order = sorted(range(self.n), key=lambda n: (n // C, n + (self.LATE + 0.5) * self.is_product[n]))
        self.place = [self.order.index(n) for n in range(self.n)]
        self.exp_order = sorted(range(len(self.units)),
                                key=lambda u: self.units[u][-1] - (self.EARLY + 0.5) * (len(self.units[u]) == 1))
        self.exp_place = [self.exp_order.index(u) for u in range(len(self.units))]

    def buffer(self, n):
        return n % self.n % SCORES

    def slot(self, n):
        n %= self.n
        same = [u for u, steps in enumerate(self.units) if (len(steps) == 1) == self.is_product[n]]
        return self.is_product[n], same.index(self.unit[n]) % (SINGLES if self.is_product[n] else self.doubles), n - self.units[self.unit[n]][0]

    def last_like(self, what, n):
        return next(m for m in range(n - 1, n - 2 * self.n, -1) if what(m) == what(n))

    def all_before(self, i, n):
        return self.n * i + n

    def of_kind_before(self, i, n, product):
        per_body = sum(x == product for x in self.is_product)
        ahead, n = divmod(n, self.n)
        return per_body * i + per_body * ahead + sum(x == product for x in self.is_product[:n])

    def exped_by(self, i, n):
        beside, n = divmod(n, self.n)
        return len(self.units) * i + len(self.units) * beside + self.exp_place[self.unit[n]] + 1

    def used_by(self, i, n):
        behind, n = divmod(n, self.n)
        return self.n * i + self.n * behind + self.place[n] + 1


def attend(nc, at_d, et_d, qp_d, kp_d, v_d, shift_d, o_d, over, when, products, at, prefetched):
    with ExitStack() as ctx:
        s = Scope(nc, ctx, f"at{when}")
        plan = Steps(products)
        doubles = [s.sb(f"double{k}", [P, 2, NB]) for k in range(plan.doubles)]
        singles = [s.sb(f"single{k}", [P, 1, NB]) for k in range(SINGLES if products else 0)]
        q = [s.sb(f"q{k}", [P, NB], BF16) for k in range(2)]
        k_all = [s.sb(f"k{k}", [P, NP], BF16) for k in range(2)]
        v = [s.sb(f"v{k}", [P, C, VW]) for k in range(2)]
        o = [s.sb(f"o{k}", [P, QW]) for k in range(2)]
        score = [s.ps(f"score{k}", [P, -(-NB // BANK) * BANK]) for k in range(SCORES)]
        acc = [s.ps(f"acc{k}", [P, BANK]) for k in range(2)]
        cleared, k_zero = s.sem("cleared"), s.sem("k_zero")
        at_loaded = [s.sem(f"at_loaded{g}") for g in range(-(-C // CHUNKS_AT_ONCE) + 1)]
        head_loaded = [s.sem(f"head_loaded{k}") for k in range(2)]
        scored = s.sem("scored")
        added = s.sem("added")
        exped = s.sem("exped")
        multiplied = s.sem("multiplied")
        used = s.sem("used")
        kept = s.sem("kept")
        stored = [s.sem(f"stored{k}") for k in range(2)]
        block = ctx.enter_context(nc.Block())
        STEPS = plan.n
        UNITS = len(plan.units)
        AHEAD = STEPS
        BODIES = HEADS // GROUP
        LOADS = 16 * (PARTS + PARTS * PARTS + 1 + 3)
        STORES = 16 * COLT
        CLEARED = 8
        SCORE_LEAD = 8
        KEEP_LAG = 5
        assert GROUP * products % SINGLES == 0 and GROUP % 2 == 0

        first_of_group = {steps[0]: g for g, steps in enumerate(plan.groups)}

        def slot(n):
            product, buffer, half = plan.slot(n)
            return (singles if product else doubles)[buffer][:, half, :]

        def runs(eng):
            return eng.If(eng.value_load(over[0:1, 0:1], min_val=0, max_val=1) == when)

        @block.sync
        def _(sp):
            def load_adjacency(b, which):
                for g in which:
                    last = plan.groups[g][-1]
                    if b:
                        sp.wait_ge(multiplied if plan.is_product[last] else added,
                                   plan.of_kind_before(b * BODIES - 1, STEPS - C + last + 1, plan.is_product[last]))
                    load_group(sp, at_d, et_d, at, plan, g, b, at_loaded[g])

            def load(b, d, k):
                load_products(sp, qp_d, kp_d, d * N + b * NB, NB, q[k], d * N, N, k_all[k], head_loaded[k])
                sp.dma_start(q[k][SHIFT_ROW:SHIFT_ROW + PARTS, :],
                             bass.AP(shift_d, d * NP + b * NB, [[HEADS * NP, PARTS], [1, NB]])).then_inc(head_loaded[k], 16)
                sp.dma_start(v[k][:, 0:C - 1, :].rearrange("p j w -> p (j w)"),
                             bass.AP(v_d, d * (N * VW), [[C * VW, P], [1, (C - 1) * VW]])).then_inc(head_loaded[k], 16)
                for x, y in row_pieces(LAST):
                    sp.dma_start(v[k][x:y, C - 1, :], bass.AP(v_d, d * (N * VW) + (x * C + C - 1) * VW,
                                                              [[C * VW, y - x], [1, VW]])).then_inc(head_loaded[k], 16)

            def store(b, d, k):
                sp.wait_ge(kept, d + (b * HEADS + 1 + 2))
                for t in range(COLT):
                    width = min(QW, N - b * NB - t * QW)
                    sp.dma_start(bass.AP(o_d, d * N + (b * NB + t * QW), [[TOK, VW], [1, width]]),
                                 o[k][32 * t:32 * t + VW, 0:width]).then_inc(stored[k], 16)

            with runs(sp):
                for k in range(2):
                    sp.sem_inc(stored[k], STORES)
                sp.wait_ge(prefetched, 16 * len(Steps(PRODUCTS).prefetched))
                if products:
                    for g in plan.prefetched:
                        sp.sem_inc(at_loaded[g], 16)
                else:
                    load_adjacency(0, plan.prefetched)
                sp.wait_ge(cleared, CLEARED)
                for k in range(2):
                    load(0, k, k)
                load_adjacency(0, [g for g in range(len(plan.groups)) if g not in plan.prefetched])
                for b in range(BLOCKS):
                    with sp.Fori(0, HEADS // 2 - 1) as i:
                        for k in range(2):
                            sp.wait_ge(used, i * (2 * C) + ((b * HEADS + k + 1) * C + AHEAD))
                            load(b, 2 * i + (k + 2), k)
                            store(b, 2 * i + k, k)
                    for k in range(2):
                        if b + 1 < BLOCKS:
                            sp.wait_ge(used, ((b + 1) * HEADS - 1 + k) * C + AHEAD)
                            load(b + 1, k, k)
                            if k == 0:
                                load_adjacency(b + 1, range(len(plan.groups)))
                        store(b, HEADS - 2 + k, k)
                for k in range(2):
                    sp.wait_ge(stored[k], STORES * (BLOCKS * HEADS // 2 + 1))

        @block.gpsimd
        def _(pool):
            with runs(pool):
                pool.memset(k_all[1][:], 0.0).then_inc(k_zero, 1)
                if not products:
                    return
                for b in range(BLOCKS):
                    with pool.Fori(0, BODIES) as i:
                        for n in range(STEPS):
                            if plan.is_product[n]:
                                if n in first_of_group:
                                    pool.wait_ge(at_loaded[first_of_group[n]], 16 * (b + 1))
                                pool.wait_ge(exped, plan.exped_by(i, n) + b * BODIES * UNITS)
                                pool.tensor_tensor(slot(n), slot(n), at[:, plan.chunk[n], :],
                                                   ALU.mult).then_inc(multiplied, 1)

        @block.tensor
        def _(pe):
            def scores(i, n):
                head, step = divmod(n % STEPS, C)
                k = head % 2
                if step == 0:
                    pe.wait_ge(head_loaded[k], LOADS * (GROUP // 2) * i + LOADS * (n // C // 2 + 1))
                if not (isinstance(i, int) and i == 0 and n < SCORES):
                    m = plan.last_like(plan.buffer, n)
                    if plan.is_product[m % STEPS]:
                        pe.wait_ge(exped, plan.exped_by(i, m))
                    else:
                        pe.wait_ge(added, plan.of_kind_before(i, m + 1, False))
                keys = k_all[k][:].rearrange("r (p j) -> r j p", j=C)[:, plan.chunk[n % STEPS], :]
                for a, b in col_pieces(NB):
                    last = pe.matmul(score[plan.buffer(n)][:, a:b], keys, q[k][:, a:b], start=True, stop=True)
                last.then_inc(scored, 1)

            def values(i, m):
                n = plan.order[m]
                head = n // C
                k = head % 2
                if m % C == 0:
                    pe.wait_ge(kept, GROUP * i + (head + 1))
                if plan.is_product[n]:
                    pe.wait_ge(multiplied, plan.of_kind_before(i, n + 1, True))
                else:
                    pe.wait_ge(exped, plan.exped_by(i, n))
                for t in range(COLT):
                    last = pe.matmul(acc[k][32 * t:32 * t + VW, 0:QW], v[k][:, plan.chunk[n % STEPS], :],
                                     slot(n)[:, t * QW:(t + 1) * QW],
                                     start=(m % C == 0), stop=(m % C == C - 1), tile_position=(0, 32 * t))
                last.then_inc(used, 1)

            def body(i, more):
                for n in range(STEPS):
                    if n + SCORE_LEAD < STEPS or more:
                        scores(i, n + SCORE_LEAD)
                    values(i, n)

            with runs(pe):
                pe.sem_inc(used, AHEAD)
                pe.wait_ge(cleared, CLEARED)
                for n in range(SCORE_LEAD):
                    scores(0, n)
                with pe.Fori(0, BLOCKS * BODIES - 1) as i:
                    body(i, True)
                body(BLOCKS * BODIES - 1, False)

        @block.vector
        def _(dve):
            with runs(dve):
                dve.memset(k_all[0][:], 0.0).then_inc(k_zero, 1)
                for k in range(2):
                    dve.memset(q[k][:], 0.0).then_inc(cleared, 1)
                    dve.memset(v[k][:, C - 1, :], 0.0).then_inc(cleared, 1)
                    dve.memset(acc[k][:, 0:QW], 0.0).then_inc(cleared, 1)
                dve.wait_ge(k_zero, 2)
                for k in range(2):
                    dve.memset(k_all[k][SHIFT_ROW:SHIFT_ROW + PARTS, 0:N], 1.0).then_inc(cleared, 1)
                for b in range(BLOCKS):
                    with dve.Fori(0, BODIES) as i:
                        for n in range(STEPS):
                            if not plan.is_product[n]:
                                if n in first_of_group:
                                    dve.wait_ge(at_loaded[first_of_group[n]], 16 * (b + 1))
                                dve.wait_ge(scored, plan.all_before(i, n) + (b * BODIES * STEPS + 1))
                                dve.wait_ge(used, plan.used_by(i, plan.last_like(plan.slot, n)) + (b * BODIES * STEPS + AHEAD))
                                dve.scalar_tensor_tensor(out=slot(n), in0=at[:, plan.chunk[n], :], scalar=2.0,
                                                         in1=score[plan.buffer(n)][:, 0:NB], op0=ALU.mult, op1=ALU.add).then_inc(added, 1)

        @block.scalar
        def _(act):
            def exponential(i, m):
                ahead, m = divmod(m, UNITS)
                steps = [n + ahead * STEPS for n in plan.units[plan.exp_order[m]]]
                product, buffer, _ = plan.slot(steps[0])
                if product:
                    n = steps[0]
                    act.wait_ge(scored, plan.all_before(i, n + 1))
                    act.wait_ge(used, plan.used_by(i, plan.last_like(plan.slot, n)) + AHEAD)
                    act.activation(slot(n), score[plan.buffer(n)][:, 0:NB], ACT.Exp).then_inc(exped, 1)
                else:
                    act.wait_ge(added, plan.of_kind_before(i, steps[-1] + 1, False))
                    act.activation(doubles[buffer][:], doubles[buffer][:], ACT.Exp).then_inc(exped, 1)

            def keep_head(i, head):
                act.wait_ge(used, STEPS * i + ((head + 1) * C + AHEAD))
                act.wait_ge(stored[head % 2], STORES * (GROUP // 2) * i + STORES * (head // 2 + 1))
                act.activation(o[head % 2][:], acc[head % 2][:, 0:QW], ACT.Copy).then_inc(kept, 1)

            def body(i, more):
                for m in range(KEEP_LAG, UNITS + KEEP_LAG):
                    if m < UNITS or more:
                        exponential(i, m)
                    if m % (UNITS // GROUP) == KEEP_LAG - 1:
                        keep_head(i, m // (UNITS // GROUP) - 1)

            with runs(act):
                act.sem_inc(kept, 2)
                for m in range(KEEP_LAG):
                    exponential(0, m)
                with act.Fori(0, BLOCKS * BODIES - 1) as i:
                    body(i, True)
                body(BLOCKS * BODIES - 1, False)


def project_out(nc, o_d, out, keep):
    with ExitStack() as ctx:
        s = Scope(nc, ctx, "po")
        raw = [s.sb(f"raw{k}", [P, VW, P]) for k in range(2)]
        inv = s.sb("inv", [P, P])
        scaled = [s.sb(f"scaled{k}", [P, H, P]) for k in range(2)]
        turned = [s.sb(f"turned{k}", [P, H, P]) for k in range(2)]
        result = [s.sb(f"result{k}", [P, F]) for k in range(2)]
        tp = [s.ps(f"tp{k}", [P, H, P]) for k in range(2)]
        py = [s.ps(f"py{k}", [P, BANK]) for k in range(2)]
        loaded = [s.sem(f"loaded{k}") for k in range(2)]
        stored, result_free = s.sem("stored"), s.sem("result_free")
        cleared, inverted, divided, turned_ready, turned_kept, product, added = [
            s.sem(n) for n in ("cleared", "inverted", "divided", "turned_ready", "turned_kept", "product", "added")]
        block = ctx.enter_context(nc.Block())

        def rows_of(c):
            return LAST if isinstance(c, int) and c == C - 1 else P

        @block.sync
        def _(sp):
            def load(c, k):
                sp.wait_ge(divided, c + 1)
                for a, b in ([(0, P)] if rows_of(c) == P else row_pieces(LAST)):
                    sp.dma_start(raw[k][a:b, :, :], bass.AP(o_d, c * (P * P) + a * P, [[P, b - a], [TOK, VW], [1, P]])).then_inc(loaded[k], 16)

            sp.wait_ge(cleared, 2)
            with sp.Fori(0, C // 2 - 1) as i:
                for k in range(2):
                    load(2 * i + k, k)
            for c in (C - 2, C - 1):
                load(c, c % 2)

        @block.gpsimd
        def _(pool):
            def store(c, k):
                pool.wait_ge(added, c + 3)
                r = rows_of(c)
                pool.dma_start(bass.AP(out.tensor, c * (P * F), [[F, r], [1, F]]), result[k][0:r, :]).then_inc(stored, 16)
                pool.wait_ge(stored, 16 * c + 16)
                pool.sem_inc(result_free, 1)

            pool.sem_inc(result_free, 2)
            with pool.Fori(0, C // 2 - 1) as i:
                for k in range(2):
                    store(2 * i + k, k)
            for c in (C - 2, C - 1):
                store(c, c % 2)

        @block.tensor
        def _(pe):
            def turn(c, k):
                pe.wait_ge(divided, c + 3)
                pe.wait_ge(turned_kept, c + 1)
                for h in range(H):
                    last = pe.transpose(tp[k][:, h, :], scaled[k][:, h, :], keep["ident"][:])
                last.then_inc(turned_ready, 1)

            def project_back(c, k):
                pe.wait_ge(turned_kept, c + 3)
                pe.wait_ge(added, c + 1)
                for h in range(H):
                    last = pe.matmul(py[k][:, 0:F], turned[k][:, h, :], keep["wo_t"][:, h, :], start=(h == 0), stop=(h == H - 1))
                last.then_inc(product, 1)

            pe.sem_inc(turned_ready, 2)
            pe.sem_inc(product, 2)
            turn(0, 0)
            with pe.Fori(0, C // 2 - 1) as i:
                for k in range(2):
                    turn(2 * i + k + 1, 1 - k)
                    project_back(2 * i + k, k)
            turn(C - 1, 1)
            project_back(C - 2, 0)
            project_back(C - 1, 1)

        @block.scalar
        def _(act):
            def keep_turned(c, k):
                act.wait_ge(turned_ready, c + 3)
                act.wait_ge(product, c + 1)
                act.activation(turned[k][:], tp[k][:], ACT.Copy).then_inc(turned_kept, 1)

            act.sem_inc(turned_kept, 2)
            keep_turned(0, 0)
            with act.Fori(0, C // 2 - 1) as i:
                for k in range(2):
                    keep_turned(2 * i + k + 1, 1 - k)
            keep_turned(C - 1, 1)

        @block.vector
        def _(dve):
            dve.sem_inc(divided, 2)
            dve.sem_inc(added, 2)
            for k in range(2):
                dve.memset(raw[k][:], 1.0).then_inc(cleared, 1)

            def divide(c, k, count):
                dve.wait_ge(loaded[k], count)
                dve.wait_ge(divided, c + 2)
                dve.reciprocal(inv[:], raw[k][:, H, :]).then_inc(inverted, 1)
                dve.wait_ge(inverted, c + 1)
                dve.wait_ge(turned_ready, c + 1)
                dve.tensor_tensor(scaled[k][:], raw[k][:, 0:H, :], inv[:].unsqueeze(1).to_broadcast([P, H, P]),
                                  ALU.mult).then_inc(divided, 1)

            def add(c, k):
                dve.wait_ge(product, c + 3)
                dve.wait_ge(result_free, c + 1)
                dve.tensor_tensor(result[k][:], py[k][:, 0:F], keep["x"][:, c, :], ALU.add).then_inc(added, 1)

            for k in range(2):
                divide(k, k, 16)
            with dve.Fori(0, C // 2 - 2) as i:
                for k in range(2):
                    divide(2 * i + k + 2, k, 16 * i + 32)
                    add(2 * i + k, k)
            for c in range(C - 4, C):
                if c + 2 < C:
                    divide(c + 2, c % 2, 16 * ((c + 2) // 2 + 1) + (16 if c + 2 == C - 1 else 0))
                add(c, c % 2)


def gnn_two_layers(nc, x, adj, w_in, w_out, wq, wk, wv, wo, out):
    at_d = nc.dram_tensor("adj_t_scratch", (P, C, NP), F32)
    et_d = nc.dram_tensor("exp_adj_t_scratch", (P, PRODUCTS, NP), F32)
    amax_d = nc.dram_tensor("amax_scratch", (NP,), F32)
    qp_d = nc.dram_tensor("q_parts_scratch", (PARTS, H, TOK), BF16)
    kp_d = nc.dram_tensor("k_parts_scratch", (PARTS, H, TOK), BF16)
    v_d = nc.dram_tensor("v_scratch", (TOK, VW), F32)
    nq_d = nc.dram_tensor("q_norm_scratch", (TOK,), F32)
    nk_d = nc.dram_tensor("k_norm_scratch", (TOK,), F32)
    shift_d = nc.dram_tensor("shift_scratch", (PARTS, HEADS, NP), BF16)
    o_d = nc.dram_tensor("attended_scratch", (VW, TOK), F32)
    with ExitStack() as ctx:
        s = Scope(nc, ctx, "all")
        keep = {"x": s.sb("x", [P, C, F]), "ident": s.sb("ident", [P, P]), "ones": s.sb("ones", [P, 1]),
                "wo_t": s.sb("wo_t", [P, H, P])}
        over = s.sb("over", [1, 1], I32)
        with ExitStack() as early:
            e = Scope(nc, early, "early")
            keep |= {"h_nat": e.sb("h_nat", [P, C, F]), "w_t": e.sb("w_t", [P, 3 * H * P]), "h_t": e.sb("h_t", [P, NP])}
            with ExitStack() as layer:
                y = Scope(nc, layer, "layer1")
                keep |= {"h_int": y.sb("h_int", [P, C, F]), "in_acc": y.sb("in_acc", [P, NP]),
                         "out_acc": y.sb("out_acc", [P, NP]), "col_acc": y.sb("col_acc", [P, NP]),
                         "row_sum": y.sb("row_sum", [P, C])}
                load_and_norm_first(nc, x, keep)
                stream_adjacency(nc, adj, at_d, et_d, amax_d, keep)
                finish_first_layer(nc, w_in, w_out, wq, wk, wv, wo, keep)
            project(nc, qp_d, kp_d, v_d, nq_d, nk_d, keep)
        with ExitStack() as attention:
            a = Scope(nc, attention, "attention")
            at = a.sb("adj_t", [P, C, NB])
            prefetched = a.sem("prefetched")
            with ExitStack() as middle:
                m = Scope(nc, middle, "softmax")
                shift = m.sb("shift", [P, NP])
                bound_scores(nc, nq_d, nk_d, amax_d, shift, over, keep["ident"], at, at_d, et_d, prefetched)
                take_true_maxima(nc, adj, qp_d, kp_d, shift, over, keep["ident"])
                split_shift(nc, shift, shift_d)
            attend(nc, at_d, et_d, qp_d, kp_d, v_d, shift_d, o_d, over, 0, PRODUCTS, at, prefetched)
            attend(nc, at_d, et_d, qp_d, kp_d, v_d, shift_d, o_d, over, 1, 0, at, prefetched)
        project_out(nc, o_d, out, keep)


_INS = ["x", "adj", "L0_gnn_W_in", "L0_gnn_W_out", "L1_gnn_Wq", "L1_gnn_Wk", "L1_gnn_Wv", "L1_gnn_Wo"]
_OUTS = [((N, F), "float32")]


def kernel(**inputs):
    import numpy as _np
    import concourse.bacc as _bacc
    from concourse import mybir as _mybir
    from concourse.bass_utils import run_bass_kernel_spmd as _run

    nc = _bacc.Bacc("TRN2", target_bir_lowering=False, num_devices=1)
    arrays, args = {}, []
    for name in _INS:
        a = _np.ascontiguousarray(inputs[name])
        arrays[f"in_{name}_dram"] = a
        args.append(nc.dram_tensor(f"in_{name}_dram", a.shape, _mybir.dt.from_np(a.dtype), kind="ExternalInput").ap())
    for i, (shape, dtype) in enumerate(_OUTS):
        dt = _mybir.dt.from_np(_np.dtype(dtype))
        args.append(nc.dram_tensor(f"out_{i}_dram", shape, dt, kind="ExternalOutput").ap())
    gnn_two_layers(nc, *args)
    r = _run(nc, [arrays], core_ids=[0])
    got = tuple(r.results[0][f"out_{i}_dram"] for i in range(len(_OUTS)))
    return got[0]
```
